# Optimizing a Trainium2 kernel written in Bass

```python
import numpy as np
import jax
import jax.numpy as jnp

def _softmax(x, axis=-1):
    return jax.nn.softmax(x, axis=axis)
def _gelu(x):
    return jax.nn.gelu(x, approximate=True)
def _silu(x):
    return jax.nn.silu(x)
def _sigmoid(x):
    return jax.nn.sigmoid(x)
def _layernorm(x, axis=-1, eps=1e-5):
    m = jnp.mean(x, axis=axis, keepdims=True)
    v = jnp.var(x, axis=axis, keepdims=True)
    return (x - m) / jnp.sqrt(v + eps)
def _scatter_add(tgt, idx, src, axis=0):
    return tgt.at[idx].add(src)
def _segment_sum(src, seg, n):
    return jax.ops.segment_sum(src, seg, n)

kernel_name = 'mk_conv_preact_d2_conv_nhwc384_e50372'

def setup_inputs(seed: int = 0):
    np.random.seed(seed)
    _w = jnp.asarray
    def _rec_inputs():
        import jax
        import jax.numpy as jnp
        _gk = jax.random.key(seed)
        x = -0.000357 + 1 * jax.random.normal(jax.random.fold_in(_gk, 1), (16, 56, 56, 384), jnp.float32)
        return x
    x = _rec_inputs()
    def _L0_conv_setup():
        import jax, jax.numpy as jnp
        import numpy as np
        SHIFT_SIZE = 5
        PAD = SHIFT_SIZE // 2

        def _shift_list(pad, C):
            base = list(range(-pad, pad + 1)) + list(range(pad - 1, -pad, -1))
            n = C // len(base) + 1
            return (base * n)[:C]

        def cycle_shift_vertical(x, pad):
            B, C, H, W = x.shape
            shifts = jnp.array(_shift_list(pad, C))
            padded = jnp.pad(x, ((0, 0), (0, 0), (pad, pad), (0, 0)))
            row_idx = pad + jnp.arange(H)[None, :] - shifts[:, None]
            return jnp.take_along_axis(padded, row_idx[None, :, :, None], axis=2)
        key = jax.random.key(seed)
        ks = jax.random.split(key, 11)
        B, H, W, C = (16, 56, 56, 384)
        Cq = C // 4
        s = lambda k, shp, fan: jax.random.normal(k, shp, jnp.float32) * (1.0 / np.sqrt(fan))
        return {'x': jax.random.normal(ks[0], (B, H, W, C), jnp.float32), 'w_h': s(ks[1], (C, C), C), 'b_h': jnp.zeros((C,), jnp.float32), 'w_c': s(ks[2], (C, C), C), 'b_c': jnp.zeros((C,), jnp.float32), 'w_r1': s(ks[3], (C, Cq), C), 'b_r1': jnp.zeros((Cq,), jnp.float32), 'w_r2': s(ks[4], (Cq, 3 * C), Cq), 'b_r2': jnp.zeros((3 * C,), jnp.float32), 'w_p': s(ks[5], (C, C), C), 'b_p': jnp.zeros((C,), jnp.float32)}
    _L0_conv_all = _L0_conv_setup()
    _L0_conv_in = {k: v for k, v in _L0_conv_all.items() if k in ('w_h', 'b_h', 'w_c', 'b_c', 'w_r1', 'b_r1', 'w_r2', 'b_r2', 'w_p', 'b_p', )}
    del _L0_conv_all

    def _L1_conv_setup():
        import jax, jax.numpy as jnp
        import numpy as np
        WINDOW = (1, 5, 20)
        FILL = 1.0

        def box_sum(x, axis, w):
            if w == 1:
                return x
            lo = w // 2
            hi = w - lo - 1
            xm = jnp.moveaxis(x, axis, -1)
            shp = xm.shape
            xr = xm.reshape(-1, 1, shp[-1])
            k = jnp.ones((1, 1, w), x.dtype)
            y = jax.lax.conv_general_dilated(xr, k, window_strides=(1,), padding=[(lo, hi)])
            return jnp.moveaxis(y.reshape(shp), -1, axis)
        key = jax.random.key(seed)
        x = jax.random.normal(key, (2, 256, 256, 384), dtype=jnp.float32)
        return {'x': x}
    _L1_conv_all = _L1_conv_setup()
    _L1_conv_in = {k: v for k, v in _L1_conv_all.items() if k in ()}
    del _L1_conv_all

    return {
        "x": x,
        "L0_conv_w_h": _L0_conv_in["w_h"],
        "L0_conv_b_h": _L0_conv_in["b_h"],
        "L0_conv_w_c": _L0_conv_in["w_c"],
        "L0_conv_b_c": _L0_conv_in["b_c"],
        "L0_conv_w_r1": _L0_conv_in["w_r1"],
        "L0_conv_b_r1": _L0_conv_in["b_r1"],
        "L0_conv_w_r2": _L0_conv_in["w_r2"],
        "L0_conv_b_r2": _L0_conv_in["b_r2"],
        "L0_conv_w_p": _L0_conv_in["w_p"],
        "L0_conv_b_p": _L0_conv_in["b_p"],
    }

def reference(x, L0_conv_w_h, L0_conv_b_h, L0_conv_w_c, L0_conv_b_c, L0_conv_w_r1, L0_conv_b_r1, L0_conv_w_r2, L0_conv_b_r2, L0_conv_w_p, L0_conv_b_p):
    import jax
    import jax.numpy as jnp
    def _L0_conv_ref(x, w_h, b_h, w_c, b_c, w_r1, b_r1, w_r2, b_r2, w_p, b_p):
        import jax, jax.numpy as jnp
        import numpy as np
        SHIFT_SIZE = 5
        PAD = SHIFT_SIZE // 2

        def _shift_list(pad, C):
            base = list(range(-pad, pad + 1)) + list(range(pad - 1, -pad, -1))
            n = C // len(base) + 1
            return (base * n)[:C]

        def cycle_shift_vertical(x, pad):
            B, C, H, W = x.shape
            shifts = jnp.array(_shift_list(pad, C))
            padded = jnp.pad(x, ((0, 0), (0, 0), (pad, pad), (0, 0)))
            row_idx = pad + jnp.arange(H)[None, :] - shifts[:, None]
            return jnp.take_along_axis(padded, row_idx[None, :, :, None], axis=2)
        B, H, W, C = x.shape
        xs = cycle_shift_vertical(jnp.transpose(x, (0, 3, 1, 2)), PAD)
        xs = jnp.transpose(xs, (0, 2, 3, 1))
        x_h = xs @ w_h + b_h
        x_w = x_h
        x_c = x @ w_c + b_c
        a = jnp.mean(x_h + x_w + x_c, axis=(1, 2))
        a = jax.nn.gelu(a @ w_r1 + b_r1, approximate=False) @ w_r2 + b_r2
        a = a.reshape(B, C, 3).transpose(2, 0, 1)
        a = jax.nn.softmax(a, axis=0)[:, :, None, None, :]
        out = x_h * a[0] + x_w * a[1] + x_c * a[2]
        return out @ w_p + b_p

    def _L1_conv_ref(x):
        import jax, jax.numpy as jnp
        import numpy as np
        WINDOW = (1, 5, 20)
        FILL = 1.0

        def box_sum(x, axis, w):
            if w == 1:
                return x
            lo = w // 2
            hi = w - lo - 1
            xm = jnp.moveaxis(x, axis, -1)
            shp = xm.shape
            xr = xm.reshape(-1, 1, shp[-1])
            k = jnp.ones((1, 1, w), x.dtype)
            y = jax.lax.conv_general_dilated(xr, k, window_strides=(1,), padding=[(lo, hi)])
            return jnp.moveaxis(y.reshape(shp), -1, axis)
        w0, w1, w2 = WINDOW
        s = box_sum(box_sum(x, 1, w0), 2, w1)
        num = box_sum(s * s, 3, w2)
        d = box_sum(box_sum(box_sum(x * x, 1, w0), 2, w1), 3, w2)
        c0 = box_sum(jnp.ones((x.shape[1],), x.dtype), 0, w0)
        c1 = box_sum(jnp.ones((x.shape[2],), x.dtype), 0, w1)
        norm = c0[:, None] * c1[None, :]
        denum = d * norm[None, :, :, None]
        return jnp.nan_to_num(num / denum, nan=FILL)

    def _gn(v, G=32, eps=1e-5):
        B_, H_, W_, C_ = v.shape
        g = v.reshape(B_, H_, W_, G, C_ // G)
        m = jnp.mean(g, axis=(1, 2, 4), keepdims=True)
        s = jnp.var(g, axis=(1, 2, 4), keepdims=True)
        return ((g - m) / jnp.sqrt(s + eps)).reshape(v.shape)

    def _ln_c(v, eps=1e-6):
        m = jnp.mean(v, axis=-1, keepdims=True)
        s = jnp.var(v, axis=-1, keepdims=True)
        return (v - m) / jnp.sqrt(s + eps)

    def _ln_t(v, eps=1e-5):
        m = jnp.mean(v, axis=-1, keepdims=True)
        s = jnp.var(v, axis=-1, keepdims=True)
        return (v - m) / jnp.sqrt(s + eps)

    def _to_tokens(v):
        B_, H_, W_, C_ = v.shape
        return v.reshape(B_, H_ * W_, C_)
    def _from_tokens(t, like):
        return t.reshape(like.shape)

    x = x + _L0_conv_ref(_gn(x), L0_conv_w_h, L0_conv_b_h, L0_conv_w_c, L0_conv_b_c, L0_conv_w_r1, L0_conv_b_r1, L0_conv_w_r2, L0_conv_b_r2, L0_conv_w_p, L0_conv_b_p)
    x = x + _L1_conv_ref(_gn(x))
    return x


_drawn_inputs = setup_inputs


def setup_inputs(seed=0):
    import zlib

    import numpy as np

    out = dict(_drawn_inputs(seed))
    spreads = {'L0_conv_b_h': (0.0, 0.1),
     'L0_conv_b_c': (0.0, 0.1),
     'L0_conv_b_r1': (0.0, 0.523),
     'L0_conv_b_r2': (0.0, 0.1),
     'L0_conv_b_p': (0.0, 0.1)}
    factors = {}
    for name, (base, spread) in spreads.items():
        noise = np.random.default_rng([zlib.crc32(name.encode()), seed]).standard_normal(out[name].shape)
        drawn = base * np.exp(spread * noise) if base else spread * noise
        out[name] = jnp.asarray(drawn.astype(out[name].dtype))
    for name, factor in factors.items():
        out[name] = (out[name] * factor).astype(out[name].dtype)
    return out
```

```python
import numpy as np
import concourse.bass as bass
from concourse import mybir
from contextlib import ExitStack

WINDOW_W, WINDOW_C = 5, 20
SHIFT_PERIOD = 8
SHIFTS = (-2, -1, 0, 1, 2, 1, 0, -1)
GROUPS = 32
EPS = 1e-5
TINY = 2.0 ** -63
P = 128

ERF_TOP = (-2.72614225801306e-10, 2.77068142495902e-08, -2.10102402082508e-06, -5.69250639462346e-05,
           -7.34990630326855e-04, -2.95459980854025e-03, -1.60960333262415e-02)
ERF_LOW = (0.0, 0.0, -1.45660718464996e-05, -2.13374055278905e-04, -1.68282697438203e-03,
           -7.37332916720468e-03, -1.42647390514189e-02)


def geometry(shape):
    B, H, W, C = shape
    g = dict(B=B, H=H, W=W, C=C, KT=C // P, NPX=H * W, ROWS=8, TPX=2 * W)
    g["PITCH"] = W + 2
    g["OPX"] = 2 * g["PITCH"] - 2
    g["CHUNKS"] = H // g["ROWS"]
    g["CPX"] = g["ROWS"] * W
    g["TILES"] = g["CPX"] // g["TPX"]
    return g


def bands(C):
    lo, hi = WINDOW_C // 2, WINDOW_C - WINDOW_C // 2 - 1
    return [(max(0, k - hi), min(C, k + P + lo)) for k in range(0, C, P)]


def constant_blob(g):
    C, KT, W, H = g["C"], g["KT"], g["W"], g["H"]
    lo, hi = WINDOW_C // 2, WINDOW_C - WINDOW_C // 2 - 1
    parts, at, n = [], {}, 0

    def put(name, a):
        nonlocal n
        full = np.zeros((P, a.shape[1]), np.float32)
        full[:a.shape[0]] = a
        parts.append(full)
        at[name] = (n, n + a.shape[1])
        n += a.shape[1]

    put("ident", np.eye(P))
    c = np.arange(C)
    per = C // GROUPS
    same = (c[:, None] // per == c[None, :] // per) / np.float64(per)
    for k in range(KT):
        for m in range(KT):
            put(f"group{k}{m}", same[k * P:(k + 1) * P, m * P:(m + 1) * P])
    box = ((c[:, None] >= c[None, :] - lo) & (c[:, None] <= c[None, :] + hi)).astype(np.float64)
    for k, (a, b) in enumerate(bands(C)):
        put(f"band{k}", box[k * P:(k + 1) * P, a:b])
    w = np.minimum(np.arange(g["OPX"]) % g["PITCH"], W - 1)
    taps = np.minimum(w + WINDOW_W // 2, W - 1) - np.maximum(w - WINDOW_W // 2, 0) + 1
    put("taps", taps[:, None])
    s = np.array(SHIFTS)[np.arange(P) % SHIFT_PERIOD]
    lost = np.stack([s <= -1, s <= -2, s >= 2, s >= 1], 1).astype(np.float64)
    put("lost", lost / (H * W))
    put("lost_share", (lost.sum(1) / H)[:, None])
    put("erf", np.repeat(np.stack([ERF_TOP, ERF_LOW], 1).reshape(1, -1), P, 0))
    return np.ascontiguousarray(np.concatenate(parts, 1)), at


class Steps:

    def __init__(self, eng, sem, per_image, image):
        self.eng, self.sem, self.per, self.base, self.k = eng, sem, per_image, per_image * image, 0

    def __call__(self, ins):
        self.k += 1
        ins.then_inc(self.sem, 1)

    def settle(self):
        self.eng.wait_ge(self.sem, self.base + self.k)

    def then(self, ins):
        self(ins)
        self.settle()

    def end(self):
        assert self.k == self.per, (self.k, self.per)


def build(nc, g, at, x, w_h, b_h, w_c, b_c, w_r1, b_r1, w_r2, b_r2, w_p, b_p, blob, out):
    f32, f16 = mybir.dt.float32, mybir.dt.float16
    ALU, ACT, AX = mybir.AluOpType, mybir.ActivationFunctionType, mybir.AxisListType
    B, H, W, C, KT, NPX = (g[k] for k in ("B", "H", "W", "C", "KT", "NPX"))
    ROWS, TPX, CHUNKS, CPX, TILES = (g[k] for k in ("ROWS", "TPX", "CHUNKS", "CPX", "TILES"))
    CQ = w_r1.shape[1]
    BANDS = bands(C)
    BANK = 512
    HALO = 2 * W
    PITCH, OPX = g["PITCH"], g["OPX"]
    PR = KT * ROWS
    LEAD = 5
    WS = 64.0
    GM = KT * CHUNKS
    CT = CHUNKS * TILES
    NF = 2 * KT
    SLOT = (0, 1, 2, 0, 1, 2, 3)
    SLOTS = 4
    USES = [SLOT.count(s) for s in range(SLOTS)]
    NRES = SHIFT_PERIOD
    XG0, XG1 = 17, 9
    XH, XA = 14, 8

    x_v = x.rearrange("b h w c -> b (h w) c").rearrange("b (n t p) c -> b n p t c", p=TPX, t=TILES)
    out_v = out.rearrange("b (n t r) w c -> b n t r w c", r=2, t=TILES)

    ctx = ExitStack()
    with ctx:
        def sb(name, shape, dt=f32):
            return ctx.enter_context(nc.sbuf_tensor(name, shape, dt))

        def sem(name):
            return ctx.enter_context(nc.semaphore(name))

        cst = sb("cst", [P, blob.shape[1]])
        whT = sb("whT", [P, KT, C])
        wcT = sb("wcT", [P, KT, C])
        wp = sb("wp", [P, KT, C])
        wA = sb("wA", [P, KT, C])
        wB = sb("wB", [P, KT, C])
        wr2 = sb("wr2", [CQ, KT * P * 3])
        r_h = sb("r_h", [P, KT, CQ])
        r_c = sb("r_c", [P, KT, CQ])
        cols = sb("cols", [P, 3, KT])
        br1 = sb("br1", [CQ, 1])
        br2 = sb("br2", [P, KT, 3])
        hconst = sb("hconst", [CQ, 1])
        w16 = sb("w16", [P, NF, 2, C], f16)
        xin = [sb(f"xin{s}", [TPX, TILES, C]) for s in range(2)]
        hl = sb("hl", [P, KT, 2, NPX + 2 * HALO], f16)
        sh = sb("sh", [P, SLOTS, KT, 2, CPX + 2], f16)
        x1T = sb("x1T", [P, KT, H * PITCH])
        xg = sb("xg", [P, LEAD + PR * PITCH + 3])
        q = sb("q", [P, LEAD + PR * PITCH + 3])
        s2 = [sb(f"s2_{s}", [P, PR * PITCH]) for s in range(2)]
        qw = [sb(f"qw_{s}", [P, PR * PITCH]) for s in range(2)]
        rec = sb("rec", [OPX, 2, C])
        rat = sb("rat", [OPX, 2, C])
        outb = sb("outb", [OPX, TILES, C])
        st0 = sb("st0", [P, KT, CHUNKS, 6])
        st1 = sb("st1", [P, KT, CHUNKS, 6])
        mv0 = sb("mv0", [P, KT, 2])
        mv1 = sb("mv1", [P, KT, 2])
        gs0 = sb("gs0", [P, KT, 2])
        gs1 = sb("gs1", [P, KT, 2])
        tmp0 = sb("tmp0", [P, KT])
        tmp1 = sb("tmp1", [P, KT])
        var0 = sb("var0", [P, KT])
        var1 = sb("var1", [P, KT])
        rs0 = sb("rs0", [P, KT])
        rs1 = sb("rs1", [P, KT])
        lnv0 = sb("lnv0", [P, KT])
        lnv1 = sb("lnv1", [P, KT])
        nb1 = sb("nb1", [P, KT])
        sd0 = sb("sd0", [P, KT])
        r64 = sb("r64", [P, KT])
        rowp = sb("rowp", [P, KT, 2, 2, 2])
        rows = sb("rows", [P, KT, 4])
        hx = sb("hx", [P, 2, KT])
        padv = sb("padv", [P, KT, 2], f16)
        hp = sb("hp", [CQ, 8])
        ef = sb("ef", [CQ, 2])
        gel = sb("gel", [CQ, 1])
        al = sb("al", [P, KT, 3])
        mx = sb("mx", [P, KT])
        sm = sb("sm", [P, KT])
        gA = sb("gA", [P, KT])
        gB = sb("gB", [P, KT])
        u = sb("u", [P, KT])
        u2 = sb("u2", [P, KT])
        bsum = sb("bsum", [P, KT])
        yb = sb("yb", [P, KT])
        tinyc = sb("tinyc", [P, 1])

        ps_m = [ctx.enter_context(nc.psum_tensor(f"ps_m{s}", [P, BANK], f32)) for s in range(2)]
        ps_num = [ctx.enter_context(nc.psum_tensor(f"ps_num{s}", [P, BANK], f32)) for s in range(2)]
        ps_den = [ctx.enter_context(nc.psum_tensor(f"ps_den{s}", [P, BANK], f32)) for s in range(2)]
        ps_x1 = ctx.enter_context(nc.psum_tensor("ps_x1", [P, BANK], f32))
        ps_p = ctx.enter_context(nc.psum_tensor("ps_p", [P, BANK], f32))

        def k(name, parts=P):
            a, b = at[name]
            return cst[0:parts, a:b]

        ident = k("ident")
        stat_ps = ps_p[:, 0:2 * KT].rearrange("p (m s) -> p m s", s=2)
        h_ps = ps_p[0:CQ, 16:17]
        a_ps = ps_p[:, 32:32 + 3 * KT].rearrange("p (m s) -> p m s", s=3)
        b_ps = ps_p[:, 48:48 + KT]
        stat1_ps = ps_x1[:, 0:2 * KT].rearrange("p (m s) -> p m s", s=2)

        def padded(t):
            return t[:, LEAD - 2:LEAD - 2 + PR * PITCH].rearrange("p (r w) -> p r w", w=PITCH)[:, :, 2:PITCH]

        def summed(t):
            return t[:, :].rearrange("p (r w) -> p r w", w=PITCH)[:, :, 2:PITCH]

        def x1_rows(kt, c):
            a = c * ROWS * PITCH
            return x1T[:, kt, a:a + ROWS * PITCH].rearrange("p (r w) -> p r w", w=PITCH)[:, :, 0:W]

        s_const = sem("const_loaded")
        s_w = sem("weights_loaded")
        s_zero = sem("zeros_written")
        s_sT = sem("setup_transposed")
        s_sTc = sem("setup_copied")
        s_sR = sem("setup_products")
        s_sRc = sem("setup_products_copied")
        s_x = [sem(f"x_loaded{s}") for s in range(2)]
        s_p = sem("x_transposed")
        s_hi = sem("x_high_written")
        s_pf = sem("x_low_and_stats_written")
        s_sh = [sem(f"shifted_loaded{s}") for s in range(SLOTS)]
        s_pad = sem("pads_written")
        s_c0 = sem("x_stat_steps")
        s_c1 = sem("x1_stat_steps")
        s_ch = sem("gelu_steps")
        s_ca = sem("softmax_steps")
        s_erf = sem("erf_steps")
        s_bs = sem("bias_steps")
        s_m0 = sem("x_moments")
        s_m1 = sem("x1_moments")
        s_g0 = sem("x_group_moments")
        s_g1 = sem("x1_group_moments")
        s_v0 = sem("x_variance")
        s_v1 = sem("x1_variance")
        s_l0 = sem("x_log")
        s_l1 = sem("x1_log")
        s_r0 = sem("x_rstd_first")
        s_r1 = sem("x1_rstd_first")
        s_hx = sem("means_ready")
        s_h = sem("hidden_product")
        s_gel = sem("gelu_ready")
        s_a = sem("logits")
        s_am = sem("logits_less_max")
        s_ae = sem("exponentials")
        s_g = sem("gates_ready")
        s_wA = sem("gated_weights")
        s_b = sem("bias_product")
        s_br = sem("bias_read")
        s_f = sem("fold_product")
        s_fd = sem("fold_diagonal")
        s_fh = sem("fold_high")
        s_fl = sem("fold_low")
        s_mm = sem("projected")
        s_yb = sem("bias_ready")
        s_me = sem("x1_written")
        s_st1 = sem("x1_stats_written")
        s_n1 = sem("norm1_ready")
        s_xg = sem("xg_written")
        s_q = sem("squares_written")
        s_s = sem("row_sums_written")
        s_qw = sem("square_sums_written")
        s_s2 = sem("squared_sums_written")
        s_den = sem("den_ready")
        s_num = sem("num_ready")
        s_xp = sem("x1_back")
        s_ln = sem("log_written")
        s_rec = sem("reciprocal_written")
        s_rat = sem("ratio_written")
        s_out = sem("out_written")
        s_st = [sem(f"out_stored{t}") for t in range(TILES)]

        def wait(eng, s, value):
            if isinstance(value, int) and value <= 0:
                return
            eng.wait_ge(s, value)

        def items(c_too, m_too, p_too):
            if c_too:
                yield "norm1", 0, 0
                yield "prep", 0, 0
            if m_too:
                yield "norm0", 0, 0
            if c_too:
                yield "prep", 1, 0
                yield "tile", 0, 0
                yield "tile", 0, 1
            if m_too:
                yield "hidden", 0, 0
            if c_too:
                yield "tile", 0, 2
                yield "tile", 0, 3
            if m_too:
                yield "gate", 0, 0
            if c_too:
                yield "tile", 1, 0
                yield "tile", 1, 1
            if m_too:
                yield "bias", 0, 0
            if c_too:
                yield "prep", 2, 0
                yield "tile", 1, 2
                yield "tile", 1, 3
            if m_too:
                for f in range(NF):
                    yield "fold", f, 0
            for c in range(CHUNKS):
                if c_too and c + 3 < CHUNKS:
                    yield "prep", c + 3, 0
                for n in range(KT):
                    if m_too:
                        yield "project", c, n
                    if p_too and c:
                        yield "read", c - 1, n
                    if c_too and c + 2 < CHUNKS:
                        yield "tile", c + 2, n
                        if n == KT - 1:
                            yield "tile", c + 2, n + 1
            if p_too:
                for n in range(KT):
                    yield "read", CHUNKS - 1, n

        def rounds(eng, do, first=0):
            for c in range(CHUNKS):
                for n in range(KT):
                    do(("read", c, n), -1)
            for it in items(False, True, True):
                do(it, 0)
            for it in items(True, True, True):
                do(it, 1)
            with eng.Fori(2, B - 1) as i:
                for it in items(True, True, True):
                    do(it, i)
            for it in items(True, True, False):
                do(it, B - 1)
            for it in items(True, False, False):
                do(it, B)

        block = ctx.enter_context(nc.Block())

        @block.sync
        def _(sp):
            sp.dma_start(cst[:, :], blob).then_inc(s_const, 16)
            n = 0
            for dst, src in ((wA, w_h), (wB, w_c), (wp, w_p)):
                sp.dma_start(dst[:, :, :], src.rearrange("(t p) n -> p t n", p=P)).then_inc(s_w, 16)
            sp.dma_start(s2[0][:, 0:KT * CQ].rearrange("p (t n) -> p t n", t=KT),
                         w_r1.rearrange("(t p) n -> p t n", p=P)).then_inc(s_w, 16)
            sp.dma_start(wr2[:, :], w_r2).then_inc(s_w, 16)
            for n, b in enumerate((b_h, b_c, b_p)):
                sp.dma_start(cols[:, n, :], b.rearrange("(t p) -> p t", p=P),
                             allow_slow_non_contiguous=True).then_inc(s_w, 16)
            sp.dma_start(br1[:, :], b_r1.rearrange("(p o) -> p o", o=1), allow_slow_non_contiguous=True).then_inc(s_w, 16)
            sp.dma_start(br2[:, :, :], b_r2.rearrange("(t p s) -> p t s", p=P, s=3)).then_inc(s_w, 16)
            for c in range(2):
                sp.dma_start(xin[c][:, :, :], x_v[0, c]).then_inc(s_x[c], 16)

            def shift(i, c):
                prev = [d for d in range(c) if SLOT[d] == SLOT[c]]
                if prev:
                    wait(sp, s_mm, GM * i + KT * (prev[-1] + 1))
                else:
                    last = max(d for d in range(CHUNKS) if SLOT[d] == SLOT[c])
                    wait(sp, s_mm, GM * (i - 1) + KT * (last + 1))
                for r in range(NRES):
                    a = HALO + c * CPX - SHIFTS[r] * W
                    sp.dma_start(sh[r:P:NRES, SLOT[c], :, :, 2:2 + CPX],
                                 hl[r:P:NRES, :, :, a:a + CPX]).then_inc(s_sh[SLOT[c]], 16)

            def do(it, i):
                what, c, n = it
                if what == "norm0":
                    if not isinstance(i, int) or i < B - 1:
                        sp.wait_ge(s_p, GM * (i + 1))
                        for d in range(2):
                            sp.dma_start(xin[d][:, :, :], x_v[i + 1, d]).then_inc(s_x[d], 16)
                    sp.wait_ge(s_pad, i + 1)
                    for d in (0, 1, 2, 6):
                        shift(i, d)
                elif what == "project" and n == KT - 1 and c < 3:
                    shift(i, c + 3)
                elif what == "read" and n == KT - 1:
                    img = i + 1
                    if c + 2 < CHUNKS:
                        sp.wait_ge(s_p, GM * img + KT * (c + 1))
                        sp.dma_start(xin[c % 2][:, :, :], x_v[img, c + 2]).then_inc(s_x[c % 2], 16)
                elif what == "tile":
                    j = i - 1
                    sp.wait_ge(s_out, CT * j + TILES * c + n + 1)
                    for r in range(2):
                        sp.dma_start(out_v[j, c, n, r],
                                     outb[r * PITCH:r * PITCH + W, n, :]).then_inc(s_st[n], 16)

            rounds(sp, do)
            for t in range(TILES):
                sp.wait_ge(s_st[t], 2 * 16 * CHUNKS * B)

        @block.gpsimd
        def _(pool):
            nc.gpsimd.memset(xg[:, :], 0.0).then_inc(s_zero, 1)
            nc.gpsimd.memset(q[:, :], 0.0).then_inc(s_zero, 1)
            nc.gpsimd.memset(tinyc[:, :], TINY).then_inc(s_zero, 1)
            gaps = x1T[:, :, :].rearrange("p t (h w) -> p (t h) w", w=PITCH)[:, :, W:PITCH]
            nc.gpsimd.memset(gaps, 0.0).then_inc(s_zero, 1)

            def do(it, i):
                if it[0] == "gate":
                    pool.wait_ge(s_g, i + 1)
                    wait(pool, s_f, NF * i)
                    if isinstance(i, int) and i == 0:
                        pool.wait_ge(s_sTc, 2 * KT)
                    for gate, dst in ((gA, wA), (gB, wB)):
                        for kt in range(KT):
                            nc.gpsimd.tensor_tensor(dst[:, kt, :], wp[:, kt, :],
                                                    gate[:, kt:kt + 1].to_broadcast([P, C]),
                                                    ALU.mult).then_inc(s_wA, 1)

            rounds(pool, do)

        def free_shift(eng, i, c):
            if isinstance(i, int) and i < 0:
                return
            for d in ((0, c) if c == 1 else (c,)):
                if d < CHUNKS:
                    nth = sum(1 for e in range(d) if SLOT[e] == SLOT[d])
                    eng.wait_ge(s_sh[SLOT[d]], 16 * NRES * (USES[SLOT[d]] * i + nth + 1))

        def rstd_start(act, s_v, s_l, s_r, var, lnv, rs, i):
            act.wait_ge(s_v, i + 1)
            nc.scalar.activation(lnv[:, :], var[:, :], ACT.Ln).then_inc(s_l, 1)
            act.wait_ge(s_l, i + 1)
            nc.scalar.activation(rs[:, :], lnv[:, :], ACT.Exp, scale=-0.5).then_inc(s_r, 1)

        @block.scalar
        def _(act):
            nc.scalar.preload_act_table_set("natural_log_exp_and_others")
            act.wait_ge(s_zero, 4)
            for n in range(2 * KT):
                act.wait_ge(s_sT, n + 1)
                dst = (whT, wcT)[n // KT]
                nc.scalar.copy(dst[:, n % KT, :], ps_m[n % 2][:, 0:C]).then_inc(s_sTc, 1)

            def do(it, i):
                what, c, n = it
                if what == "norm0":
                    rstd_start(act, s_v0, s_l0, s_r0, var0, lnv0, rs0, i)
                elif what == "norm1":
                    rstd_start(act, s_v1, s_l1, s_r1, var1, lnv1, rs1, i - 1)
                elif what == "gate":
                    act.wait_ge(s_am, i + 1)
                    nc.scalar.activation(al[:, :, :], al[:, :, :], ACT.Exp).then_inc(s_ae, 1)
                elif what == "fold":
                    if c < KT:
                        act.wait_ge(s_f, NF * i + c + 1)
                    else:
                        act.wait_ge(s_fd, KT * i + c - KT + 1)
                    nc.scalar.activation(w16[:, c, 0, :], ps_m[c % 2][:, 0:C], ACT.Copy,
                                         scale=r64[:, c % KT:c % KT + 1]).then_inc(s_fh, 1)
                elif what == "read":
                    img = i + 1
                    act.wait_ge(s_p, GM * img + KT * c + n + 1)
                    if n == 0:
                        wait(act, s_mm, GM * i + KT * (c + 1))
                        free_shift(act, i, c + 1)
                    nc.scalar.copy(hl[:, n, 0, HALO + c * CPX:HALO + (c + 1) * CPX],
                                   ps_p[:, 0:CPX]).then_inc(s_hi, 1)
                elif what == "project":
                    m = KT * c + n
                    act.wait_ge(s_mm, GM * i + m + 1)
                    if c == 0:
                        act.wait_ge(s_yb, KT * i + n + 1)
                    if n == 0:
                        wait(act, s_xg, KT * (CHUNKS * (i - 1) + c + 1))
                        wait(act, s_xp, CT * (i - 1) + TILES * (c + 1))
                    a = 1 if c == 0 else 0
                    nc.scalar.activation(x1_rows(n, c), ps_m[m % 2][:, a:a + CPX].rearrange("p (r w) -> p r w", w=W),
                                         ACT.Identity, bias=yb[:, n:n + 1], scale=1.0 / WS).then_inc(s_me, 1)
                elif what == "prep":
                    j = i - 1
                    done = CHUNKS * j + c
                    act.wait_ge(s_xg, KT * (done + 1))
                    wait(act, s_qw, done)
                    nc.scalar.activation(padded(q), padded(xg), ACT.Square).then_inc(s_q, 1)
                    act.wait_ge(s_s, done + 1)
                    v = summed(s2[c % 2])
                    nc.scalar.activation(v, v, ACT.Square).then_inc(s_s2, 1)
                elif what == "tile":
                    j = i - 1
                    done = CT * j + TILES * c + n
                    act.wait_ge(s_den, done + 1)
                    wait(act, s_rat, CT * j + max(0, TILES * c + n - 1))
                    r = rec[:, n % 2, :]
                    nc.scalar.activation(r, ps_den[n % 2][0:OPX, 0:C], ACT.Ln, bias=tinyc[0:OPX, :],
                                         scale=k("taps", OPX)).then_inc(s_ln, 1)
                    act.wait_ge(s_ln, done + 1)
                    nc.scalar.activation(r, r, ACT.Exp, scale=-1.0).then_inc(s_rec, 1)

            rounds(act, do)

        def newton(step, var, rs, tmp):
            step.then(nc.vector.tensor_tensor(tmp[:, :], rs[:, :], rs[:, :], ALU.mult))
            step.then(nc.vector.tensor_tensor(tmp[:, :], tmp[:, :], var[:, :], ALU.mult))
            step.then(nc.vector.tensor_scalar(tmp[:, :], tmp[:, :], -0.5, 1.5, ALU.mult, ALU.add))
            step.then(nc.vector.tensor_tensor(rs[:, :], rs[:, :], tmp[:, :], ALU.mult))

        @block.vector
        def _(dve):
            dve.wait_ge(s_w, 16 * 10)
            dve.wait_ge(s_const, 16)
            nc.vector.tensor_scalar(tmp0[:, :], cols[:, 0, :], 2.0, None, ALU.mult).then_inc(s_sRc, 1)
            dve.wait_ge(s_sRc, 1)
            nc.vector.tensor_tensor(tmp0[:, :], tmp0[:, :], cols[:, 1, :], ALU.add).then_inc(s_sRc, 1)
            for n in range(2 * KT):
                dve.wait_ge(s_sR, n + 1)
                dst, f = ((r_h, 2.0), (r_c, 1.0))[n // KT]
                nc.vector.tensor_scalar(dst[:, n % KT, :], ps_num[n % 2][:, 0:CQ], f, None,
                                        ALU.mult).then_inc(s_sRc, 1)
            dve.wait_ge(s_sR, 2 * KT + 1)
            nc.vector.tensor_tensor(hconst[:, :], ps_x1[0:CQ, 0:1], br1[:, :], ALU.add).then_inc(s_sRc, 1)
            dve.wait_ge(s_sRc, 2 * KT + 3)
            dve.wait_ge(s_zero, 4)

            gelu_steps = [None]

            def moments(step, st, mv, tmp):
                for kt in range(KT):
                    step(nc.vector.bn_aggr(mv[:, kt, :], st[:, kt, :, :].rearrange("p c s -> p (c s)")))
                step.settle()
                step.then(nc.vector.tensor_tensor(tmp[:, :], mv[:, :, 0], mv[:, :, 0], ALU.mult))

            def do(it, i):
                what, c, n = it
                if what == "read":
                    img = i + 1
                    m = GM * img + KT * c + n
                    dve.wait_ge(s_hi, m + 1)
                    a = HALO + c * CPX
                    nc.vector.tensor_tensor(hl[:, n, 1, a:a + CPX], ps_p[:, 0:CPX], hl[:, n, 0, a:a + CPX],
                                            ALU.subtract)
                    nc.vector.bn_stats(st0[:, n, c, :], ps_p[:, 0:CPX]).then_inc(s_pf, 1)
                elif what == "norm0":
                    step = Steps(dve, s_c0, XG0, i)
                    dve.wait_ge(s_pf, GM * (i + 1))
                    nc.vector.memset(tmp0[:, :], 0.0)
                    moments(step, st0, mv0, tmp0)
                    nc.vector.tensor_tensor(mv0[:, :, 1], mv0[:, :, 1], tmp0[:, :], ALU.add).then_inc(s_m0, 1)
                    for e, a in ((0, HALO), (1, HALO + NPX - 2 * W)):
                        for kt in range(KT):
                            ins = nc.vector.tensor_reduce(
                                rowp[:, kt, :, e, :],
                                hl[:, kt, :, a:a + 2 * W].rearrange("p s (r w) -> p s r w", w=W), AX.X, ALU.add)
                            if kt == KT - 1:
                                step(ins)
                    step.settle()
                    step.then(nc.vector.tensor_tensor(
                        rows[:, :, :], rowp[:, :, 0].rearrange("p t e r -> p t (e r)"),
                        rowp[:, :, 1].rearrange("p t e r -> p t (e r)"), ALU.add))
                    for kt in range(KT):
                        ins = nc.vector.tensor_tensor(rows[:, kt, :], rows[:, kt, :], k("lost"), ALU.mult)
                    step.then(ins)
                    step.then(nc.vector.tensor_reduce(tmp0[:, :], rows[:, :, :], AX.X, ALU.add))
                    dve.wait_ge(s_g0, i + 1)
                    step.then(nc.vector.tensor_copy(gs0[:, :, :], stat_ps))
                    step.then(nc.vector.tensor_copy(padv[:, :, 0], gs0[:, :, 0]))
                    step.then(nc.vector.tensor_tensor(padv[:, :, 1], gs0[:, :, 0], padv[:, :, 0], ALU.subtract))
                    step.then(nc.vector.tensor_tensor(var0[:, :], gs0[:, :, 0], gs0[:, :, 0], ALU.mult))
                    step.then(nc.vector.tensor_tensor(var0[:, :], gs0[:, :, 1], var0[:, :], ALU.subtract))
                    nc.vector.tensor_scalar(var0[:, :], var0[:, :], 0.0, EPS, ALU.max, ALU.add).then_inc(s_v0, 1)
                    wait(dve, s_mm, GM * i)
                    if not (isinstance(i, int) and i == 0):
                        for s in range(SLOTS):
                            dve.wait_ge(s_sh[s], 16 * NRES * USES[s] * i)
                    for kt in range(KT):
                        for a in (0, HALO + NPX):
                            nc.vector.tensor_copy(hl[:, kt, :, a:a + HALO],
                                                  padv[:, kt, :].unsqueeze(2).to_broadcast([P, 2, HALO]))
                    nc.vector.tensor_copy(sh[:, 0, :, :, 1:2],
                                          padv[:, :, :].unsqueeze(3)).then_inc(s_pad, 1)
                    step.then(nc.vector.tensor_tensor(hx[:, 1, :], mv0[:, :, 0], gs0[:, :, 0], ALU.subtract))
                    step.then(nc.vector.tensor_tensor(hx[:, 0, :], hx[:, 1, :], tmp0[:, :], ALU.subtract))
                    step.then(nc.vector.scalar_tensor_tensor(hx[:, 0, :], gs0[:, :, 0], k("lost_share"),
                                                             hx[:, 0, :], ALU.mult, ALU.add))
                    dve.wait_ge(s_r0, i + 1)
                    step2 = Steps(dve, s_ch, XH, i)
                    newton(step2, var0, rs0, tmp0)
                    for s in range(2):
                        ins = nc.vector.tensor_tensor(hx[:, s, :], hx[:, s, :], rs0[:, :], ALU.mult)
                    ins.then_inc(s_hx, 1)
                    step2(nc.vector.tensor_tensor(sd0[:, :], var0[:, :], rs0[:, :], ALU.mult))
                    step2(nc.vector.tensor_scalar(r64[:, :], rs0[:, :], WS, None, ALU.mult))
                    step.end()
                    gelu_steps[0] = step2
                elif what == "hidden":
                    step = gelu_steps[0]
                    dve.wait_ge(s_h, i + 1)
                    step.then(nc.vector.tensor_tensor(hp[:, 0:1], h_ps, hconst[:, :], ALU.add))
                    step.then(nc.vector.tensor_scalar(hp[:, 1:2], hp[:, 0:1], 0.5 ** 0.5, 4.0, ALU.mult, ALU.min))
                    step.then(nc.vector.tensor_scalar(hp[:, 1:2], hp[:, 1:2], -4.0, None, ALU.max))
                    step.then(nc.vector.tensor_tensor(hp[:, 2:3], hp[:, 1:2], hp[:, 1:2], ALU.mult))
                    coef = k("erf", CQ).rearrange("p (k s) -> p k s", s=2)
                    src = coef[:, 0, :]
                    for t in range(1, len(ERF_TOP)):
                        ins = nc.vector.scalar_tensor_tensor(ef[:, :], src, hp[:, 2:3], coef[:, t, :],
                                                             ALU.mult, ALU.add)
                        ins.then_inc(s_erf, 1)
                        dve.wait_ge(s_erf, (len(ERF_TOP) - 1) * i + t)
                        src = ef[:, :]
                    step.then(nc.vector.reciprocal(hp[:, 3:4], ef[:, 1:2]))
                    step.then(nc.vector.tensor_tensor(hp[:, 4:5], ef[:, 0:1], hp[:, 1:2], ALU.mult))
                    step.then(nc.vector.tensor_tensor(hp[:, 4:5], hp[:, 4:5], hp[:, 3:4], ALU.mult))
                    step.then(nc.vector.tensor_scalar(hp[:, 4:5], hp[:, 4:5], 1.0, 0.5, ALU.add, ALU.mult))
                    nc.vector.tensor_tensor(gel[:, :], hp[:, 4:5], hp[:, 0:1], ALU.mult).then_inc(s_gel, 1)
                    step.end()
                elif what == "gate":
                    step = Steps(dve, s_ca, XA, i)
                    dve.wait_ge(s_a, i + 1)
                    step.then(nc.vector.tensor_tensor(al[:, :, :], a_ps, br2[:, :, :], ALU.add))
                    step.then(nc.vector.tensor_reduce(mx[:, :], al[:, :, :], AX.X, ALU.max))
                    for s in range(3):
                        ins = nc.vector.tensor_tensor(al[:, :, s], al[:, :, s], mx[:, :], ALU.subtract)
                    ins.then_inc(s_am, 1)
                    dve.wait_ge(s_ae, i + 1)
                    step(nc.vector.tensor_reduce(sm[:, :], al[:, :, :], AX.X, ALU.add))
                    step.then(nc.vector.tensor_tensor(gA[:, :], al[:, :, 0], al[:, :, 1], ALU.add))
                    step.then(nc.vector.reciprocal(sm[:, :], sm[:, :]))
                    nc.vector.tensor_tensor(gA[:, :], gA[:, :], sm[:, :], ALU.mult)
                    nc.vector.tensor_tensor(gB[:, :], al[:, :, 2], sm[:, :], ALU.mult).then_inc(s_g, 1)
                    dve.wait_ge(s_g, i + 1)
                    step(nc.vector.tensor_tensor(u[:, :], gA[:, :], cols[:, 0, :], ALU.mult))
                    step.then(nc.vector.tensor_tensor(u2[:, :], gB[:, :], cols[:, 1, :], ALU.mult))
                    step(nc.vector.tensor_tensor(u[:, :], u[:, :], u2[:, :], ALU.add))
                    step.end()
                elif what == "bias":
                    dve.wait_ge(s_b, i + 1)
                    nc.vector.tensor_tensor(bsum[:, :], b_ps, cols[:, 2, :], ALU.add).then_inc(s_bs, 1)
                    dve.wait_ge(s_bs, i + 1)
                    nc.vector.tensor_tensor(bsum[:, :], bsum[:, :], gs0[:, :, 0], ALU.add).then_inc(s_br, 1)
                elif what == "fold":
                    m = ps_m[c % 2]
                    if c >= KT:
                        dve.wait_ge(s_f, NF * i + c + 1)
                        kt = c - KT
                        d = m[:, kt * P:(kt + 1) * P]
                        nc.vector.scalar_tensor_tensor(d, ident, sd0[:, kt:kt + 1], d, ALU.mult,
                                                       ALU.add).then_inc(s_fd, 1)
                    dve.wait_ge(s_fh, NF * i + c + 1)
                    nc.vector.scalar_tensor_tensor(w16[:, c, 1, :], m[:, 0:C], r64[:, c % KT:c % KT + 1],
                                                   w16[:, c, 0, :], ALU.mult, ALU.subtract).then_inc(s_fl, 1)
                elif what == "project":
                    m = KT * c + n
                    if c == 0:
                        dve.wait_ge(s_mm, GM * i + m + 1)
                        wait(dve, s_me, GM * i)
                        dve.wait_ge(s_br, i + 1)
                        nc.vector.tensor_scalar(yb[:, n:n + 1], ps_m[m % 2][:, 0:1], -1.0 / WS, bsum[:, n:n + 1],
                                                ALU.mult, ALU.add).then_inc(s_yb, 1)
                    dve.wait_ge(s_me, GM * i + m + 1)
                    nc.vector.bn_stats(st1[:, n, c, :], x1_rows(n, c)).then_inc(s_st1, 1)
                elif what == "norm1":
                    j = i - 1
                    step = Steps(dve, s_c1, XG1 + 4, j)
                    dve.wait_ge(s_st1, GM * (j + 1))
                    nc.vector.memset(tmp1[:, :], 0.0)
                    moments(step, st1, mv1, tmp1)
                    nc.vector.tensor_tensor(mv1[:, :, 1], mv1[:, :, 1], tmp1[:, :], ALU.add).then_inc(s_m1, 1)
                    dve.wait_ge(s_g1, j + 1)
                    step.then(nc.vector.tensor_copy(gs1[:, :, :], stat1_ps))
                    step.then(nc.vector.tensor_tensor(var1[:, :], gs1[:, :, 0], gs1[:, :, 0], ALU.mult))
                    step.then(nc.vector.tensor_tensor(var1[:, :], gs1[:, :, 1], var1[:, :], ALU.subtract))
                    nc.vector.tensor_scalar(var1[:, :], var1[:, :], 0.0, EPS, ALU.max, ALU.add).then_inc(s_v1, 1)
                    dve.wait_ge(s_r1, j + 1)
                    newton(step, var1, rs1, tmp1)
                    step.then(nc.vector.tensor_tensor(nb1[:, :], gs1[:, :, 0], rs1[:, :], ALU.mult))
                    step(nc.vector.tensor_scalar(nb1[:, :], nb1[:, :], -1.0, None, ALU.mult))
                    step.settle()
                    step.end()
                elif what == "prep":
                    j = i - 1
                    done = CHUNKS * j + c
                    wait(dve, s_q, done)
                    wait(dve, s_s, done)
                    for kt in range(KT):
                        nc.vector.tensor_scalar(
                            padded(xg)[:, kt * ROWS:(kt + 1) * ROWS, :],
                            x1_rows(kt, c),
                            rs1[:, kt:kt + 1], nb1[:, kt:kt + 1], ALU.mult, ALU.add).then_inc(s_xg, 1)
                    dve.wait_ge(s_xg, KT * (done + 1))
                    wait(dve, s_num, CT * j + TILES * max(0, c - 1))
                    n_run = PR * PITCH
                    nc.vector.tensor_tensor_scan(s2[c % 2][:, :], xg[:, LEAD:LEAD + n_run], xg[:, 0:n_run],
                                                 0.0, ALU.add, ALU.subtract).then_inc(s_s, 1)
                    dve.wait_ge(s_q, done + 1)
                    nc.vector.tensor_tensor_scan(qw[c % 2][:, :], q[:, LEAD:LEAD + n_run], q[:, 0:n_run],
                                                 0.0, ALU.add, ALU.subtract).then_inc(s_qw, 1)
                elif what == "tile":
                    j = i - 1
                    done = CT * j + TILES * c + n
                    dve.wait_ge(s_num, done + 1)
                    dve.wait_ge(s_rec, done + 1)
                    nc.vector.scalar_tensor_tensor(rat[:, n % 2, :], ps_num[n % 2][0:OPX, 0:C], TINY,
                                                   rec[:, n % 2, :], ALU.add, ALU.mult).then_inc(s_rat, 1)
                    dve.wait_ge(s_xp, done + 1)
                    dve.wait_ge(s_rat, done + 1)
                    wait(dve, s_st[n], 2 * 16 * (CHUNKS * j + c))
                    nc.vector.tensor_tensor(outb[:, n, :], ps_x1[0:OPX, 0:C], rat[:, n % 2, :],
                                            ALU.add).then_inc(s_out, 1)

            rounds(dve, do)

        @block.tensor
        def _(pe):
            pe.wait_ge(s_const, 16)
            pe.wait_ge(s_w, 16 * 10)
            for n in range(2 * KT):
                src = (wA, wB)[n // KT]
                wait(pe, s_sTc, n - 1)
                for t in range(KT):
                    last = nc.tensor.transpose(ps_m[n % 2][:, t * P:(t + 1) * P],
                                               src[:, t, (n % KT) * P:(n % KT + 1) * P], ident)
                last.then_inc(s_sT, 1)
            pe.wait_ge(s_sTc, 2 * KT)
            wr1 = s2[0][:, 0:KT * CQ].rearrange("p (t n) -> p t n", t=KT)
            for n in range(2 * KT):
                src = (whT, wcT)[n // KT]
                wait(pe, s_sRc, n - 1 + 2)
                for t in range(KT):
                    last = nc.tensor.matmul(ps_num[n % 2][:, 0:CQ], src[:, t, (n % KT) * P:(n % KT + 1) * P],
                                            wr1[:, t, :], start=(t == 0), stop=(t == KT - 1))
                last.then_inc(s_sR, 1)
            pe.wait_ge(s_sRc, 2)
            for t in range(KT):
                last = nc.tensor.matmul(ps_x1[0:CQ, 0:1], wr1[:, t, :], tmp0[:, t:t + 1],
                                        start=(t == 0), stop=(t == KT - 1))
            last.then_inc(s_sR, 1)
            pe.wait_ge(s_sRc, 2 * KT + 3)

            def group_moments(dst, mv):
                for m in range(KT):
                    near = [t for t in range(KT) if abs(t - m) <= 1]
                    for t in near:
                        last = nc.tensor.matmul(dst[:, m, :], k(f"group{t}{m}"), mv[:, t, :],
                                                start=(t == near[0]), stop=(t == near[-1]))
                return last

            def do(it, i):
                what, c, n = it
                if what == "read":
                    img = i + 1
                    m = GM * img + KT * c + n
                    if n == 0:
                        slot = c % 2
                        per = (CHUNKS + 1 - slot) // 2
                        pe.wait_ge(s_x[slot], 16 * (per * img + c // 2 + 1))
                        if c == 0:
                            wait(pe, s_br, i + 1)
                    wait(pe, s_pf, m)
                    for t in range(TILES):
                        last = nc.tensor.transpose(ps_p[:, t * TPX:(t + 1) * TPX],
                                                   xin[c % 2][:, t, n * P:(n + 1) * P], ident[0:TPX, 0:TPX])
                    last.then_inc(s_p, 1)
                elif what == "norm0":
                    pe.wait_ge(s_m0, i + 1)
                    pe.wait_ge(s_pf, GM * (i + 1))
                    group_moments(stat_ps, mv0).then_inc(s_g0, 1)
                elif what == "norm1":
                    pe.wait_ge(s_m1, i)
                    wait(pe, s_out, CT * (i - 1))
                    group_moments(stat1_ps, mv1).then_inc(s_g1, 1)
                elif what == "hidden":
                    pe.wait_ge(s_hx, i + 1)
                    for s, r in enumerate((r_h, r_c)):
                        for t in range(KT):
                            last = nc.tensor.matmul(h_ps, r[:, t, :], hx[:, s, t:t + 1],
                                                    start=(s == 0 and t == 0), stop=(s == 1 and t == KT - 1))
                    last.then_inc(s_h, 1)
                elif what == "gate":
                    pe.wait_ge(s_gel, i + 1)
                    for m in range(KT):
                        w = wr2[:, m * 3 * P:(m + 1) * 3 * P].rearrange("p (c s) -> p c s", s=3)
                        for s in range(3):
                            last = nc.tensor.matmul(a_ps[:, m, s:s + 1], w[:, :, s], gel[:, :],
                                                    start=True, stop=True)
                    last.then_inc(s_a, 1)
                elif what == "bias":
                    pe.wait_ge(s_ca, XA * (i + 1))
                    for m in range(KT):
                        for t in range(KT):
                            last = nc.tensor.matmul(b_ps[:, m:m + 1], wp[:, t, m * P:(m + 1) * P], u[:, t:t + 1],
                                                    start=(t == 0), stop=(t == KT - 1))
                    last.then_inc(s_b, 1)
                elif what == "fold":
                    pe.wait_ge(s_wA, 2 * KT * i + (KT if c < KT else 2 * KT))
                    if c < 2:
                        wait(pe, s_me, GM * i)
                    else:
                        pe.wait_ge(s_fl, NF * i + c - 1)
                    left, right = (whT, wA) if c < KT else (wcT, wB)
                    for t in range(KT):
                        last = nc.tensor.matmul(ps_m[c % 2][:, 0:C], left[:, t, (c % KT) * P:(c % KT + 1) * P],
                                                right[:, t, :], start=(t == 0), stop=(t == KT - 1))
                    last.then_inc(s_f, 1)
                elif what == "project":
                    m = KT * c + n
                    if m < 2:
                        pe.wait_ge(s_fl, NF * (i + 1))
                    else:
                        pe.wait_ge(s_me, GM * i + m - 1)
                    if n == 0:
                        nth = sum(1 for e in range(c) if SLOT[e] == SLOT[c])
                        pe.wait_ge(s_sh[SLOT[c]], 16 * NRES * (USES[SLOT[c]] * i + nth + 1))
                        if c == 0:
                            pe.wait_ge(s_pad, i + 1)
                    e = 1 if c == 0 else 0
                    a = HALO + c * CPX
                    terms = [(f, wpart, xpart) for f in range(NF) for wpart, xpart in ((0, 0), (1, 0), (0, 1))]
                    for t, (f, wpart, xpart) in enumerate(terms):
                        kt = f % KT
                        rhs = (sh[:, SLOT[c], kt, xpart, 2 - e:2 + CPX] if f < KT
                               else hl[:, kt, xpart, a - e:a + CPX])
                        last = nc.tensor.matmul(ps_m[m % 2][:, 0:CPX + e], w16[:, f, wpart, n * P:(n + 1) * P],
                                                rhs, start=(t == 0), stop=(t == len(terms) - 1))
                    last.then_inc(s_mm, 1)
                elif what == "tile":
                    j = i - 1
                    done = CT * j + TILES * c + n
                    if n == 0:
                        pe.wait_ge(s_qw, CHUNKS * j + c + 1)
                        pe.wait_ge(s_s2, CHUNKS * j + c + 1)
                    wait(pe, s_rat, CT * j + max(0, TILES * c + n - 1))
                    for src, dst, ready in ((qw, ps_den, s_den), (s2, ps_num, s_num)):
                        for t, (lo, hi) in enumerate(BANDS):
                            a = (t * ROWS + 2 * n) * PITCH + 2
                            last = nc.tensor.matmul(dst[n % 2][0:OPX, lo:hi], src[c % 2][:, a:a + OPX],
                                                    k(f"band{t}"), start=(t == 0), stop=(t == KT - 1),
                                                    skip_group_check=True)
                        last.then_inc(ready, 1)
                    wait(pe, s_out, done)
                    if c == 0 and n == 0:
                        pe.wait_ge(s_v1, j + 1)
                    a = (c * ROWS + 2 * n) * PITCH
                    for t in range(KT):
                        last = nc.tensor.transpose(ps_x1[0:OPX, t * P:(t + 1) * P], x1T[:, t, a:a + OPX], ident)
                    last.then_inc(s_xp, 1)

            rounds(pe, do)


def kernel(x, L0_conv_w_h, L0_conv_b_h, L0_conv_w_c, L0_conv_b_c, L0_conv_w_r1, L0_conv_b_r1, L0_conv_w_r2,
           L0_conv_b_r2, L0_conv_w_p, L0_conv_b_p):
    import concourse.bacc as bacc
    from concourse.bass_utils import run_bass_kernel_spmd

    g = geometry(x.shape)
    blob, at = constant_blob(g)
    nc = bacc.Bacc("TRN2", target_bir_lowering=False, num_devices=1)
    given = dict(x=x, w_h=L0_conv_w_h, b_h=L0_conv_b_h, w_c=L0_conv_w_c, b_c=L0_conv_b_c, w_r1=L0_conv_w_r1,
                 b_r1=L0_conv_b_r1, w_r2=L0_conv_w_r2, b_r2=L0_conv_b_r2, w_p=L0_conv_w_p, b_p=L0_conv_b_p,
                 blob=blob)
    arrays, args = {}, {}
    for name, a in given.items():
        a = np.ascontiguousarray(a)
        arrays[f"in_{name}"] = a
        args[name] = nc.dram_tensor(f"in_{name}", a.shape, mybir.dt.from_np(a.dtype), kind="ExternalInput").ap()
    args["out"] = nc.dram_tensor("out_x", x.shape, mybir.dt.float32, kind="ExternalOutput").ap()
    build(nc, g, at, **args)
    return run_bass_kernel_spmd(nc, [arrays], core_ids=[0]).results[0]["out_x"]
```

```python
import numpy as np
import concourse.bass as bass
from concourse import mybir
from contextlib import ExitStack

WINDOW_W, WINDOW_C = 5, 20
SHIFT_PERIOD = 8
SHIFTS = (-2, -1, 0, 1, 2, 1, 0, -1)
GROUPS = 32
EPS = 1e-5
TINY = 2.0 ** -63
P = 128

ERF_TOP = (-2.72614225801306e-10, 2.77068142495902e-08, -2.10102402082508e-06, -5.69250639462346e-05,
           -7.34990630326855e-04, -2.95459980854025e-03, -1.60960333262415e-02)
ERF_LOW = (0.0, 0.0, -1.45660718464996e-05, -2.13374055278905e-04, -1.68282697438203e-03,
           -7.37332916720468e-03, -1.42647390514189e-02)


def geometry(shape):
    B, H, W, C = shape
    g = dict(B=B, H=H, W=W, C=C, KT=C // P, NPX=H * W, ROWS=8, TPX=2 * W)
    g["PITCH"] = W + 2
    g["OPX"] = 2 * g["PITCH"] - 2
    g["CHUNKS"] = H // g["ROWS"]
    g["CPX"] = g["ROWS"] * W
    g["TILES"] = g["CPX"] // g["TPX"]
    return g


def bands(C):
    lo, hi = WINDOW_C // 2, WINDOW_C - WINDOW_C // 2 - 1
    return [(max(0, k - hi), min(C, k + P + lo)) for k in range(0, C, P)]


def constant_blob(g):
    C, KT, W, H = g["C"], g["KT"], g["W"], g["H"]
    lo, hi = WINDOW_C // 2, WINDOW_C - WINDOW_C // 2 - 1
    blobs, at = ([], []), {}

    def put(name, a, blob=0):
        full = np.zeros((P, a.shape[1]), np.float32)
        full[:a.shape[0]] = a
        n = sum(b.shape[1] for b in blobs[blob])
        blobs[blob].append(full)
        at[name] = (n, n + a.shape[1])

    put("ident", np.eye(P))
    c = np.arange(C)
    per = C // GROUPS
    same = (c[:, None] // per == c[None, :] // per).astype(np.float64)
    for k in range(KT):
        for m in range(KT):
            if abs(k - m) <= 1:
                put(f"group{k}{m}", same[k * P:(k + 1) * P, m * P:(m + 1) * P], 1)
    box = ((c[:, None] >= c[None, :] - lo) & (c[:, None] <= c[None, :] + hi)).astype(np.float64)
    for k, (a, b) in enumerate(bands(C)):
        put(f"band{k}", box[k * P:(k + 1) * P, a:b], 1)
    w = np.minimum(np.arange(g["OPX"]) % g["PITCH"], W - 1)
    taps = np.minimum(w + WINDOW_W // 2, W - 1) - np.maximum(w - WINDOW_W // 2, 0) + 1
    put("taps", taps[:, None])
    s = np.array(SHIFTS)[np.arange(P) % SHIFT_PERIOD]
    lost = np.stack([s <= -1, s <= -2, s >= 2, s >= 1], 1).astype(np.float64)
    put("lost", lost / (H * W))
    put("lost_share", (lost.sum(1) / H)[:, None])
    put("erf", np.repeat(np.stack([ERF_TOP, ERF_LOW], 1).reshape(1, -1), P, 0))
    return [np.ascontiguousarray(np.concatenate(b, 1)) for b in blobs], at


class Steps:

    def __init__(self, eng, sem, per_image, image):
        self.eng, self.sem, self.per, self.base, self.k = eng, sem, per_image, per_image * image, 0

    def __call__(self, ins):
        self.k += 1
        ins.then_inc(self.sem, 1)

    def settle(self):
        self.eng.wait_ge(self.sem, self.base + self.k)

    def then(self, ins):
        self(ins)
        self.settle()

    def end(self):
        assert self.k == self.per, (self.k, self.per)


def build(nc, g, at, x, w_h, b_h, w_c, b_c, w_r1, b_r1, w_r2, b_r2, w_p, b_p, blob, ones, out):
    f32, f16, bf16 = mybir.dt.float32, mybir.dt.float16, mybir.dt.bfloat16
    ALU, ACT, AX = mybir.AluOpType, mybir.ActivationFunctionType, mybir.AxisListType
    B, H, W, C, KT, NPX = (g[k] for k in ("B", "H", "W", "C", "KT", "NPX"))
    ROWS, TPX, CHUNKS, CPX, TILES = (g[k] for k in ("ROWS", "TPX", "CHUNKS", "CPX", "TILES"))
    CQ = w_r1.shape[1]
    BANDS = bands(C)
    BANK = 512
    HALO = 2 * W
    PITCH, OPX = g["PITCH"], g["OPX"]
    SR = KT * 2
    SLAB = SR * PITCH
    LEAD = 5
    WS = 64.0
    GM = KT * CHUNKS
    CT = CHUNKS * TILES
    NF = 2 * KT
    SLOT = (0, 1, 2, 0, 1, 2, 3)
    SLOTS = 4
    USES = [SLOT.count(s) for s in range(SLOTS)]
    NRES = SHIFT_PERIOD
    XG0, XG1, XH, XA = 23, 18, 14, 8
    READS = (6, 5, 0, 1, 2, 3, 4)
    AHEAD = 4
    READS_LEFT = GM - KT * (CHUNKS - 1)
    STAGED = (5, 6)

    x_v = x.rearrange("b h w c -> (b h w) c").rearrange("(n t p) c -> n p t c", p=TPX, t=TILES)
    out_v = out.rearrange("b (n t r) w c -> b n t r w c", r=2, t=TILES)

    ctx = ExitStack()
    with ctx:
        def sb(name, shape, dt=f32):
            return ctx.enter_context(nc.sbuf_tensor(name, shape, dt))

        def sem(name):
            return ctx.enter_context(nc.semaphore(name))

        cst = sb("cst", [P, blob.shape[1]])
        whT = sb("whT", [P, KT, C])
        wcT = sb("wcT", [P, KT, C])
        wp = sb("wp", [P, KT, C])
        wA = sb("wA", [P, KT, C])
        wB = sb("wB", [P, KT, C])
        wr2 = sb("wr2", [CQ, KT * P * 3])
        r_h = sb("r_h", [P, KT, CQ])
        r_c = sb("r_c", [P, KT, CQ])
        cols = sb("cols", [P, 3, KT])
        br1 = sb("br1", [CQ, 1])
        br2 = sb("br2", [P, KT, 3])
        hconst = sb("hconst", [CQ, 1])
        w16 = sb("w16", [P, NF, 2, C], f16)
        xin = [sb(f"xin{s}", [TPX, TILES, C]) for s in range(2)]
        hl = sb("hl", [P, KT, 2, NPX + 2 * HALO], f16)
        sh = sb("sh", [P, SLOTS, KT, 2, CPX + 2], f16)
        x1T = sb("x1T", [P, KT, H * PITCH])
        stg = sb("stg", [P, len(STAGED), KT, 2, CPX], f16)
        xg = sb("xg", [P, LEAD + SLAB + 3])
        xq = sb("xq", [P, LEAD + SLAB + 3])
        rsum = sb("rsum", [P, 2, SLAB])
        qsum = sb("qsum", [P, 2, SLAB])
        rsp = sb("rsp", [P, AHEAD, 2, SLAB], bf16)
        qsp = sb("qsp", [P, AHEAD, 2, SLAB], bf16)
        ones32 = sb("ones32", [P, ones.shape[1]])
        wr1 = sb("wr1", [P, KT, CQ])
        rec = sb("rec", [OPX, 2, C])
        outb = sb("outb", [OPX, TILES, C])
        st0 = sb("st0", [P, KT, CHUNKS, 6])
        st1 = sb("st1", [P, KT, CHUNKS, 6])
        mv0 = sb("mv0", [P, KT, 2])
        mv1 = sb("mv1", [P, KT, 2])
        mp0 = sb("mp0", [P, KT, 3, 2], bf16)
        mp1 = sb("mp1", [P, KT, 3, 2], bf16)
        one16 = sb("one16", [P, ones.shape[1]], bf16)
        gs0 = sb("gs0", [P, KT, 2])
        gs1 = sb("gs1", [P, KT, 2])
        tmp0 = sb("tmp0", [P, KT])
        tmp1 = sb("tmp1", [P, KT])
        var0 = sb("var0", [P, KT])
        var1 = sb("var1", [P, KT])
        rs0 = sb("rs0", [P, KT])
        rs1 = sb("rs1", [P, KT])
        lnv0 = sb("lnv0", [P, KT])
        lnv1 = sb("lnv1", [P, KT])
        nb1 = sb("nb1", [P, KT])
        sd0 = sb("sd0", [P, KT])
        r64 = sb("r64", [P, KT])
        rowp = sb("rowp", [P, KT, 2, 2, 2])
        rows = sb("rows", [P, KT, 4])
        hx = sb("hx", [P, 2, KT])
        padv = sb("padv", [P, KT, 2], f16)
        hp = sb("hp", [CQ, 8])
        ef = sb("ef", [CQ, 2])
        gel = sb("gel", [CQ, 1])
        al = sb("al", [P, KT, 3])
        mx = sb("mx", [P, KT])
        sm = sb("sm", [P, KT])
        gA = sb("gA", [P, KT])
        gB = sb("gB", [P, KT])
        u = sb("u", [P, KT])
        u2 = sb("u2", [P, KT])
        bsum = sb("bsum", [P, KT])
        yb = sb("yb", [P, KT])
        tinyc = sb("tinyc", [P, 1])

        ps_m = [ctx.enter_context(nc.psum_tensor(f"ps_m{s}", [P, BANK], f32)) for s in range(2)]
        ps_num = [ctx.enter_context(nc.psum_tensor(f"ps_num{s}", [P, BANK], f32)) for s in range(2)]
        ps_den = ctx.enter_context(nc.psum_tensor("ps_den", [P, BANK], f32))
        ps_x1 = [ctx.enter_context(nc.psum_tensor(f"ps_x1{s}", [P, BANK], f32)) for s in range(2)]
        ps_p = ctx.enter_context(nc.psum_tensor("ps_p", [P, BANK], f32))

        def k(name, parts=P):
            a, b = at[name]
            return cst[0:parts, a:b]

        def k16(name):
            a, b = at[name]
            return one16[:, a:b]

        ident = k("ident")
        stat_ps = ps_p[:, 0:6 * KT].rearrange("p (m s) -> p m s", s=6)
        h_ps = ps_p[0:CQ, 24:25]
        a_ps = ps_p[:, 32:32 + 3 * KT].rearrange("p (m s) -> p m s", s=3)
        b_ps = ps_p[:, 48:48 + KT]
        stat1_ps = ps_x1[0][:, 0:6 * KT].rearrange("p (m s) -> p m s", s=6)

        def padded(t):
            return t[:, LEAD - 2:LEAD - 2 + SLAB].rearrange("p (r w) -> p r w", w=PITCH)[:, :, 2:PITCH]

        def x_chunk(c, kt, part):
            if c in STAGED:
                return stg[:, STAGED.index(c), kt, part, :]
            return hl[:, kt, part, HALO + c * CPX:HALO + (c + 1) * CPX]

        def x1_rows(kt, c):
            a = c * ROWS * PITCH
            return x1T[:, kt, a:a + ROWS * PITCH].rearrange("p (r w) -> p r w", w=PITCH)[:, :, 0:W]

        def x1_slab(kt, s):
            a = 2 * s * PITCH
            return x1T[:, kt, a:a + 2 * PITCH].rearrange("p (r w) -> p r w", w=PITCH)[:, :, 0:W]

        s_const = sem("const_loaded")
        s_w = sem("weights_loaded")
        s_zero = sem("zeros_written")
        s_sT = sem("setup_transposed")
        s_sTc = sem("setup_copied")
        s_sR = sem("setup_products")
        s_sRc = sem("setup_products_copied")
        s_x = [sem(f"x_loaded{s}") for s in range(2)]
        s_p = sem("x_transposed")
        s_hi = sem("x_high_written")
        s_pf = sem("x_low_and_stats_written")
        s_sh = [sem(f"shifted_loaded{s}") for s in range(SLOTS)]
        s_pad = sem("pads_written")
        s_c0 = sem("x_stat_steps")
        s_c1 = sem("x1_stat_steps")
        s_ch = sem("gelu_steps")
        s_ca = sem("softmax_steps")
        s_erf = sem("erf_steps")
        s_bs = sem("bias_steps")
        s_m0 = sem("x_moments")
        s_m1 = sem("x1_moments")
        s_g0 = sem("x_group_moments")
        s_g1 = sem("x1_group_moments")
        s_v0 = sem("x_variance")
        s_v1 = sem("x1_variance")
        s_l0 = sem("x_log")
        s_l1 = sem("x1_log")
        s_r0 = sem("x_rstd_first")
        s_r1 = sem("x1_rstd_first")
        s_hx = sem("means_ready")
        s_h = sem("hidden_product")
        s_gel = sem("gelu_ready")
        s_a = sem("logits")
        s_am = sem("logits_less_max")
        s_ae = sem("exponentials")
        s_g = sem("gates_ready")
        s_wA = sem("gated_weights")
        s_b = sem("bias_product")
        s_br = sem("bias_read")
        s_f = sem("fold_product")
        s_fd = sem("fold_diagonal")
        s_fh = sem("fold_high")
        s_fl = sem("fold_low")
        s_mm = sem("projected")
        s_yb = sem("bias_ready")
        s_me = sem("x1_written")
        s_st1 = sem("x1_stats_written")
        s_n1 = sem("norm1_ready")
        s_xg = sem("xg_written")
        s_s = sem("row_sums_written")
        s_q = sem("squares_written")
        s_qw = sem("square_sums_written")
        s_sh_hi = sem("sums_high_written")
        s_lo = sem("sums_low_written")
        s_stc = sem("staged_copied")
        s_den = sem("den_ready")
        s_num = sem("num_ready")
        s_xp = sem("x1_back")
        s_ln = sem("log_written")
        s_rec = sem("reciprocal_written")
        s_rat = sem("ratio_written")
        s_out = sem("out_written")
        s_st = [sem(f"out_stored{t}") for t in range(TILES)]

        def wait(eng, s, value):
            if isinstance(value, int) and value <= 0:
                return
            eng.wait_ge(s, value)

        def items(c_too, m_too, p_too):
            reads = iter([("read", r, n) for r in range(CHUNKS) for n in range(KT)])

            def read(p):
                return [next(reads)] if p_too and p else []

            def project(c, n):
                return [("project", c, n)] if m_too else []

            def keep(c, n):
                return [("keep", c, n)] if m_too and c >= 0 else []

            def gate(*names):
                return [(what, 0, 0) for what in names] if p_too else []

            def sums(what, s):
                return [(what, s, 0)] if c_too and s < CT else []

            def tile(c, t, keeps=()):
                s = TILES * c + t
                yield from sums("sums", s + AHEAD)
                yield from keeps
                yield from sums("tile", s)
                yield from sums("finish", s)
                yield from sums("square_sums", s + AHEAD)
                yield from sums("split", s + AHEAD - 1)

            def first_sums(s):
                yield from sums("sums", s)
                yield from sums("square_sums", s)
                if s:
                    yield from sums("split", s - 1)

            if c_too:
                yield "moments1", 0, 0
            if m_too:
                yield "fold", 0, 0
                yield "fold", 1, 0
            if c_too:
                yield "norm1", 0, 0
            for s in range(AHEAD):
                yield from first_sums(s)
                if m_too:
                    yield "fold", s + 2, 0
            for c in range(CHUNKS):
                last = c == CHUNKS - 1
                yield from tile(c, 0, keep(c - 1, 1))
                if last:
                    yield from gate("norm0")
                yield from read(1 <= c <= READS_LEFT)
                if c:
                    yield from project(c - 1, 2)
                yield from tile(c, 1, keep(c - 1, 2))
                yield from read(not last)
                yield from tile(c, 2)
                if last:
                    yield from gate("hidden")
                yield from project(c, 0)
                yield from read(not last)
                yield from tile(c, 3)
                yield from keep(c, 0)
                if last:
                    yield from gate("gate")
                yield from project(c, 1)
                yield from read(not last)
                if c == CHUNKS - 2:
                    yield from gate("moments0")
            yield from keep(CHUNKS - 1, 1)
            yield from gate("bias")
            yield from project(CHUNKS - 1, 2)
            yield from keep(CHUNKS - 1, 2)

        def rounds(eng, do):
            for r in range(CHUNKS):
                for n in range(KT):
                    do(("read", r, n), -1)
            for what in ("moments0", "norm0", "hidden", "gate", "bias"):
                do((what, 0, 0), -1)
            for it in items(False, True, True):
                do(it, 0)
            for it in items(True, True, True):
                do(it, 1)
            with eng.Fori(2, B - 1) as i:
                for it in items(True, True, True):
                    do(it, i)
            for it in items(True, True, False):
                do(it, B - 1)
            for it in items(True, False, False):
                do(it, B)

        block = ctx.enter_context(nc.Block())

        @block.sync
        def _(sp):
            sp.dma_start(cst[:, :], blob).then_inc(s_const, 16)
            sp.dma_start(ones32[:, :], ones).then_inc(s_const, 16)
            for dst, src in ((wA, w_h), (wB, w_c), (wp, w_p)):
                sp.dma_start(dst[:, :, :], src.rearrange("(t p) n -> p t n", p=P)).then_inc(s_w, 16)
            sp.dma_start(wr1[:, :, :], w_r1.rearrange("(t p) n -> p t n", p=P)).then_inc(s_w, 16)
            sp.dma_start(wr2[:, :], w_r2).then_inc(s_w, 16)
            for n, b in enumerate((b_h, b_c, b_p)):
                sp.dma_start(cols[:, n, :], b.rearrange("(t p) -> p t", p=P),
                             allow_slow_non_contiguous=True).then_inc(s_w, 16)
            sp.dma_start(br1[:, :], b_r1.rearrange("(p o) -> p o", o=1), allow_slow_non_contiguous=True).then_inc(s_w, 16)
            sp.dma_start(br2[:, :, :], b_r2.rearrange("(t p s) -> p t s", p=P, s=3)).then_inc(s_w, 16)
            for c in range(2):
                sp.dma_start(xin[c][:, :, :], x_v[READS[c]]).then_inc(s_x[c], 16)

            def shift(i, c):
                prev = [d for d in range(c) if SLOT[d] == SLOT[c]]
                if prev:
                    wait(sp, s_mm, GM * i + KT * (prev[-1] + 1))
                for r in range(NRES):
                    a = HALO + c * CPX - SHIFTS[r] * W
                    sp.dma_start(sh[r:P:NRES, SLOT[c], :, :, 2:2 + CPX],
                                 hl[r:P:NRES, :, :, a:a + CPX]).then_inc(s_sh[SLOT[c]], 16)

            def do(it, i):
                what, c, n = it
                if what == "fold" and c == 0:
                    wait(sp, s_mm, GM * i)
                    for n, d in enumerate(STAGED):
                        a = HALO + d * CPX
                        sp.dma_start(hl[:, :, :, a:a + CPX], stg[:, n, :, :, :]).then_inc(s_stc, 16)
                    shift(i, 1)
                    shift(i, 2)
                    if not isinstance(i, int) or i < B - 1:
                        for r in range(2):
                            sp.dma_start(xin[r][:, :, :], x_v[CHUNKS * i + (CHUNKS + READS[r])]).then_inc(s_x[r], 16)
                    sp.wait_ge(s_stc, 16 * len(STAGED) * (i + 1))
                    shift(i, 6)
                elif what == "hidden":
                    sp.wait_ge(s_pad, i + 2)
                    shift(i + 1, 0)
                elif what == "project" and n == KT - 1 and c < 3:
                    shift(i, c + 3)
                elif what == "read" and n == KT - 1 and c + 2 < CHUNKS:
                    sp.wait_ge(s_p, GM * (i + 1) + KT * (c + 1))
                    sp.dma_start(xin[c % 2][:, :, :], x_v[CHUNKS * i + (CHUNKS + READS[c + 2])]).then_inc(s_x[c % 2], 16)
                elif what == "finish":
                    j, n = i - 1, c % TILES
                    sp.wait_ge(s_out, CT * j + c + 1)
                    for r in range(2):
                        sp.dma_start(out_v[j, c // TILES, n, r],
                                     outb[r * PITCH:r * PITCH + W, n, :]).then_inc(s_st[n], 16)

            rounds(sp, do)
            for t in range(TILES):
                sp.wait_ge(s_st[t], 2 * 16 * CHUNKS * B)

        @block.gpsimd
        def _(pool):
            nc.gpsimd.memset(xg[:, :], 0.0).then_inc(s_zero, 1)
            nc.gpsimd.memset(xq[:, :], 0.0).then_inc(s_zero, 1)
            nc.gpsimd.memset(tinyc[:, :], TINY).then_inc(s_zero, 1)
            gaps = x1T[:, :, :].rearrange("p t (h w) -> p (t h) w", w=PITCH)[:, :, W:PITCH]
            nc.gpsimd.memset(gaps, 0.0).then_inc(s_zero, 1)

            def do(it, i):
                what, c, n = it
                if what == "split":
                    done = CT * (i - 1) + c
                    for h, (src, dst) in enumerate(((qsum, qsp), (rsum, rsp))):
                        pool.wait_ge(s_sh_hi, 3 * done + (1, 3)[h])
                        r = c % AHEAD
                        nc.gpsimd.tensor_tensor(dst[:, r, 1, :], src[:, c % 2, :], dst[:, r, 0, :],
                                                ALU.subtract).then_inc(s_lo, 1)
                elif what == "gate":
                    pool.wait_ge(s_g, i + 2)
                    wait(pool, s_f, NF * (i + 1))
                    if isinstance(i, int) and i < 0:
                        pool.wait_ge(s_sTc, 2 * KT)
                    for gate, dst in ((gA, wA), (gB, wB)):
                        for kt in range(KT):
                            nc.gpsimd.tensor_tensor(dst[:, kt, :], wp[:, kt, :],
                                                    gate[:, kt:kt + 1].to_broadcast([P, C]),
                                                    ALU.mult).then_inc(s_wA, 1)

            rounds(pool, do)

        def free_shift(eng, i, c):
            if isinstance(i, int) and i < 0:
                return
            for d in ((0, c) if c == 1 else (c,)):
                if d < CHUNKS:
                    nth = sum(1 for e in range(d) if SLOT[e] == SLOT[d])
                    eng.wait_ge(s_sh[SLOT[d]], 16 * NRES * (USES[SLOT[d]] * i + nth + 1))

        def rstd_start(act, s_v, s_l, s_r, var, lnv, rs, i):
            act.wait_ge(s_v, i + 1)
            nc.scalar.activation(lnv[:, :], var[:, :], ACT.Ln).then_inc(s_l, 1)
            act.wait_ge(s_l, i + 1)
            nc.scalar.activation(rs[:, :], lnv[:, :], ACT.Exp, scale=-0.5).then_inc(s_r, 1)

        @block.scalar
        def _(act):
            nc.scalar.preload_act_table_set("natural_log_exp_and_others")
            act.wait_ge(s_zero, 4)
            for n in range(2 * KT):
                act.wait_ge(s_sT, n + 1)
                dst = (whT, wcT)[n // KT]
                nc.scalar.copy(dst[:, n % KT, :], ps_m[n % 2][:, 0:C]).then_inc(s_sTc, 1)

            def do(it, i):
                what, c, n = it
                if what == "norm0":
                    rstd_start(act, s_v0, s_l0, s_r0, var0, lnv0, rs0, i + 1)
                elif what == "norm1":
                    rstd_start(act, s_v1, s_l1, s_r1, var1, lnv1, rs1, i - 1)
                elif what == "gate":
                    act.wait_ge(s_am, i + 2)
                    nc.scalar.activation(al[:, :, :], al[:, :, :], ACT.Exp).then_inc(s_ae, 1)
                elif what == "fold":
                    if c < KT:
                        act.wait_ge(s_f, NF * i + c + 1)
                    else:
                        act.wait_ge(s_fd, KT * i + c - KT + 1)
                    nc.scalar.activation(w16[:, c, 0, :], ps_m[c % 2][:, 0:C], ACT.Copy,
                                         scale=r64[:, c % KT:c % KT + 1]).then_inc(s_fh, 1)
                elif what == "read":
                    img = i + 1
                    d = READS[c]
                    act.wait_ge(s_p, GM * img + KT * c + n + 1)
                    if n == 0:
                        if d in STAGED:
                            wait(act, s_stc, 16 * len(STAGED) * img)
                        else:
                            wait(act, s_mm, GM * i + KT * (d + 1))
                            free_shift(act, i, d + 1)
                    nc.scalar.copy(x_chunk(d, n, 0), ps_p[:, 0:CPX]).then_inc(s_hi, 1)
                elif what == "keep":
                    m = KT * c + n
                    act.wait_ge(s_mm, GM * i + m + 1)
                    if c == 0:
                        act.wait_ge(s_yb, KT * i + n + 1)
                    if n == 0:
                        wait(act, s_xg, KT * (CT * (i - 1) + TILES * (c + 1)))
                        wait(act, s_xp, CT * (i - 1) + TILES * (c + 1))
                    a = 1 if c == 0 else 0
                    nc.scalar.activation(x1_rows(n, c), ps_m[m % 2][:, a:a + CPX].rearrange("p (r w) -> p r w", w=W),
                                         ACT.Identity, bias=yb[:, n:n + 1], scale=1.0 / WS).then_inc(s_me, 1)
                elif what == "square_sums":
                    done = CT * (i - 1) + c
                    act.wait_ge(s_xg, KT * (done + 1))
                    wait(act, s_qw, done)
                    nc.scalar.activation(padded(xq), padded(xg), ACT.Square).then_inc(s_q, 1)
                elif what == "split":
                    done = CT * (i - 1) + c
                    r, e = c % AHEAD, c % 2
                    act.wait_ge(s_qw, done + 1)
                    wait(act, s_num, CT * (i - 1) + max(0, c - AHEAD + 1))
                    nc.scalar.copy(qsp[:, r, 0, :], qsum[:, e, :]).then_inc(s_sh_hi, 1)
                    nc.scalar.activation(rsp[:, r, 0, :], rsum[:, e, :], ACT.Square).then_inc(s_sh_hi, 1)
                    act.wait_ge(s_sh_hi, 3 * done + 2)
                    nc.scalar.activation(rsum[:, e, :], rsum[:, e, :], ACT.Square).then_inc(s_sh_hi, 1)
                elif what == "tile":
                    j, n = i - 1, c % TILES
                    done = CT * j + c
                    act.wait_ge(s_den, done + 1)
                    wait(act, s_rat, CT * j + max(0, c - 1))
                    r = rec[:, n % 2, :]
                    nc.scalar.activation(r, ps_den[0:OPX, 0:C], ACT.Ln, bias=tinyc[0:OPX, :],
                                         scale=k("taps", OPX)).then_inc(s_ln, 1)
                    act.wait_ge(s_ln, done + 1)
                    nc.scalar.activation(r, r, ACT.Exp, scale=-1.0).then_inc(s_rec, 1)

            rounds(act, do)

        def newton(step, var, rs, tmp):
            step.then(nc.vector.tensor_tensor(tmp[:, :], rs[:, :], rs[:, :], ALU.mult))
            step.then(nc.vector.tensor_tensor(tmp[:, :], tmp[:, :], var[:, :], ALU.mult))
            step.then(nc.vector.tensor_scalar(tmp[:, :], tmp[:, :], -0.5, 1.5, ALU.mult, ALU.add))
            step.then(nc.vector.tensor_tensor(rs[:, :], rs[:, :], tmp[:, :], ALU.mult))

        @block.vector
        def _(dve):
            dve.wait_ge(s_w, 16 * 10)
            dve.wait_ge(s_const, 32)
            nc.vector.tensor_scalar(tmp0[:, :], cols[:, 0, :], 2.0, None, ALU.mult).then_inc(s_sRc, 1)
            dve.wait_ge(s_sRc, 1)
            nc.vector.tensor_tensor(tmp0[:, :], tmp0[:, :], cols[:, 1, :], ALU.add).then_inc(s_sRc, 1)
            for n in range(2 * KT):
                dve.wait_ge(s_sR, n + 1)
                dst, f = ((r_h, 2.0), (r_c, 1.0))[n // KT]
                nc.vector.tensor_scalar(dst[:, n % KT, :], ps_num[n % 2][:, 0:CQ], f, None,
                                        ALU.mult).then_inc(s_sRc, 1)
            dve.wait_ge(s_sR, 2 * KT + 1)
            nc.vector.tensor_tensor(hconst[:, :], ps_x1[0][0:CQ, 0:1], br1[:, :], ALU.add).then_inc(s_sRc, 1)
            dve.wait_ge(s_sRc, 2 * KT + 3)
            dve.wait_ge(s_zero, 4)

            chains = {}

            nc.vector.tensor_copy(one16[:, :], ones32[:, :]).then_inc(s_sRc, 1)

            def in_parts(step, mv, tmp, mp):
                step.then(nc.vector.tensor_copy(mp[:, :, 0, :], mv[:, :, :]))
                step.then(nc.vector.tensor_tensor(mv[:, :, :], mv[:, :, :], mp[:, :, 0, :], ALU.subtract))
                step.then(nc.vector.tensor_copy(mp[:, :, 1, :], mv[:, :, :]))
                return nc.vector.tensor_tensor(mp[:, :, 2, :], mv[:, :, :], mp[:, :, 1, :], ALU.subtract)

            def joined(step, gs, ps):
                step.then(nc.vector.tensor_reduce(gs[:, :, :], ps.rearrange("p m (k s) -> p m s k", s=2), AX.X,
                                                  ALU.add))
                step.then(nc.vector.tensor_scalar(gs[:, :, :], gs[:, :, :], GROUPS / C, None, ALU.mult))

            def moments(step, st, mv, tmp):
                for kt in range(KT):
                    step(nc.vector.bn_aggr(mv[:, kt, :], st[:, kt, :, :].rearrange("p c s -> p (c s)")))
                step.settle()
                step.then(nc.vector.tensor_tensor(tmp[:, :], mv[:, :, 0], mv[:, :, 0], ALU.mult))

            def do(it, i):
                what, c, n = it
                if what == "read":
                    img = i + 1
                    m = GM * img + KT * c + n
                    dve.wait_ge(s_hi, m + 1)
                    d = READS[c]
                    nc.vector.tensor_tensor(x_chunk(d, n, 1), ps_p[:, 0:CPX], x_chunk(d, n, 0), ALU.subtract)
                    nc.vector.bn_stats(st0[:, n, d, :], ps_p[:, 0:CPX]).then_inc(s_pf, 1)
                elif what == "moments0":
                    g = i + 1
                    step = Steps(dve, s_c0, XG0, g)
                    dve.wait_ge(s_pf, GM * (g + 1))
                    nc.vector.memset(tmp0[:, :], 0.0)
                    moments(step, st0, mv0, tmp0)
                    step.then(nc.vector.tensor_tensor(mv0[:, :, 1], mv0[:, :, 1], tmp0[:, :], ALU.add))
                    step.then(nc.vector.tensor_copy(hx[:, 1, :], mv0[:, :, 0]))
                    in_parts(step, mv0, tmp0, mp0).then_inc(s_m0, 1)
                    for e in range(2):
                        for kt in range(KT):
                            src = (hl[:, kt, :, HALO:HALO + 2 * W] if e == 0
                                   else stg[:, STAGED.index(CHUNKS - 1), kt, :, CPX - 2 * W:CPX])
                            ins = nc.vector.tensor_reduce(
                                rowp[:, kt, :, e, :], src.rearrange("p s (r w) -> p s r w", w=W), AX.X, ALU.add)
                            if kt == KT - 1:
                                step(ins)
                    step.settle()
                    step.then(nc.vector.tensor_tensor(
                        rows[:, :, :], rowp[:, :, 0].rearrange("p t e r -> p t (e r)"),
                        rowp[:, :, 1].rearrange("p t e r -> p t (e r)"), ALU.add))
                    for kt in range(KT):
                        ins = nc.vector.tensor_tensor(rows[:, kt, :], rows[:, kt, :], k("lost"), ALU.mult)
                    step.then(ins)
                    step.then(nc.vector.tensor_reduce(tmp0[:, :], rows[:, :, :], AX.X, ALU.add))
                    chains["x"] = step
                elif what == "norm0":
                    g = i + 1
                    step = chains["x"]
                    dve.wait_ge(s_g0, g + 1)
                    wait(dve, s_br, g)
                    joined(step, gs0, stat_ps)
                    step.then(nc.vector.tensor_copy(padv[:, :, 0], gs0[:, :, 0]))
                    step.then(nc.vector.tensor_tensor(padv[:, :, 1], gs0[:, :, 0], padv[:, :, 0], ALU.subtract))
                    step.then(nc.vector.tensor_tensor(var0[:, :], gs0[:, :, 0], gs0[:, :, 0], ALU.mult))
                    step.then(nc.vector.tensor_tensor(var0[:, :], gs0[:, :, 1], var0[:, :], ALU.subtract))
                    nc.vector.tensor_scalar(var0[:, :], var0[:, :], 0.0, EPS, ALU.max, ALU.add).then_inc(s_v0, 1)
                    step.then(nc.vector.tensor_tensor(hx[:, 1, :], hx[:, 1, :], gs0[:, :, 0], ALU.subtract))
                    step.then(nc.vector.tensor_tensor(hx[:, 0, :], hx[:, 1, :], tmp0[:, :], ALU.subtract))
                    step.then(nc.vector.scalar_tensor_tensor(hx[:, 0, :], gs0[:, :, 0], k("lost_share"),
                                                             hx[:, 0, :], ALU.mult, ALU.add))
                    dve.wait_ge(s_r0, g + 1)
                    step2 = Steps(dve, s_ch, XH, g)
                    newton(step2, var0, rs0, tmp0)
                    for s in range(2):
                        ins = nc.vector.tensor_tensor(hx[:, s, :], hx[:, s, :], rs0[:, :], ALU.mult)
                    ins.then_inc(s_hx, 1)
                    step2(nc.vector.tensor_tensor(sd0[:, :], var0[:, :], rs0[:, :], ALU.mult))
                    step2(nc.vector.tensor_scalar(r64[:, :], rs0[:, :], WS, None, ALU.mult))
                    if not (isinstance(i, int) and i < 0):
                        dve.wait_ge(s_mm, GM * i + KT)
                        for s in range(SLOTS):
                            dve.wait_ge(s_sh[s], 16 * NRES * USES[s] * g)
                    for kt in range(KT):
                        for a in (0, HALO + NPX):
                            nc.vector.tensor_copy(hl[:, kt, :, a:a + HALO],
                                                  padv[:, kt, :].unsqueeze(2).to_broadcast([P, 2, HALO]))
                    nc.vector.tensor_copy(sh[:, 0, :, :, 1:2],
                                          padv[:, :, :].unsqueeze(3)).then_inc(s_pad, 1)
                    step.end()
                    chains["gelu"] = step2
                elif what == "hidden":
                    step = chains["gelu"]
                    dve.wait_ge(s_h, i + 2)
                    step.then(nc.vector.tensor_tensor(hp[:, 0:1], h_ps, hconst[:, :], ALU.add))
                    step.then(nc.vector.tensor_scalar(hp[:, 1:2], hp[:, 0:1], 0.5 ** 0.5, 4.0, ALU.mult, ALU.min))
                    step.then(nc.vector.tensor_scalar(hp[:, 1:2], hp[:, 1:2], -4.0, None, ALU.max))
                    step.then(nc.vector.tensor_tensor(hp[:, 2:3], hp[:, 1:2], hp[:, 1:2], ALU.mult))
                    coef = k("erf", CQ).rearrange("p (k s) -> p k s", s=2)
                    src = coef[:, 0, :]
                    for t in range(1, len(ERF_TOP)):
                        ins = nc.vector.scalar_tensor_tensor(ef[:, :], src, hp[:, 2:3], coef[:, t, :],
                                                             ALU.mult, ALU.add)
                        ins.then_inc(s_erf, 1)
                        dve.wait_ge(s_erf, (len(ERF_TOP) - 1) * (i + 1) + t)
                        src = ef[:, :]
                    step.then(nc.vector.reciprocal(hp[:, 3:4], ef[:, 1:2]))
                    step.then(nc.vector.tensor_tensor(hp[:, 4:5], ef[:, 0:1], hp[:, 1:2], ALU.mult))
                    step.then(nc.vector.tensor_tensor(hp[:, 4:5], hp[:, 4:5], hp[:, 3:4], ALU.mult))
                    step.then(nc.vector.tensor_scalar(hp[:, 4:5], hp[:, 4:5], 1.0, 0.5, ALU.add, ALU.mult))
                    nc.vector.tensor_tensor(gel[:, :], hp[:, 4:5], hp[:, 0:1], ALU.mult).then_inc(s_gel, 1)
                    step.end()
                elif what == "gate":
                    step = Steps(dve, s_ca, XA, i + 1)
                    dve.wait_ge(s_a, i + 2)
                    step.then(nc.vector.tensor_tensor(al[:, :, :], a_ps, br2[:, :, :], ALU.add))
                    step.then(nc.vector.tensor_reduce(mx[:, :], al[:, :, :], AX.X, ALU.max))
                    for s in range(3):
                        ins = nc.vector.tensor_tensor(al[:, :, s], al[:, :, s], mx[:, :], ALU.subtract)
                    ins.then_inc(s_am, 1)
                    dve.wait_ge(s_ae, i + 2)
                    step(nc.vector.tensor_reduce(sm[:, :], al[:, :, :], AX.X, ALU.add))
                    step.then(nc.vector.tensor_tensor(gA[:, :], al[:, :, 0], al[:, :, 1], ALU.add))
                    step.then(nc.vector.reciprocal(sm[:, :], sm[:, :]))
                    nc.vector.tensor_tensor(gA[:, :], gA[:, :], sm[:, :], ALU.mult)
                    nc.vector.tensor_tensor(gB[:, :], al[:, :, 2], sm[:, :], ALU.mult).then_inc(s_g, 1)
                    dve.wait_ge(s_g, i + 2)
                    step(nc.vector.tensor_tensor(u[:, :], gA[:, :], cols[:, 0, :], ALU.mult))
                    step.then(nc.vector.tensor_tensor(u2[:, :], gB[:, :], cols[:, 1, :], ALU.mult))
                    step(nc.vector.tensor_tensor(u[:, :], u[:, :], u2[:, :], ALU.add))
                    step.end()
                elif what == "bias":
                    dve.wait_ge(s_b, i + 2)
                    wait(dve, s_yb, KT * (i + 1))
                    nc.vector.tensor_tensor(bsum[:, :], b_ps, cols[:, 2, :], ALU.add).then_inc(s_bs, 1)
                    dve.wait_ge(s_bs, i + 2)
                    nc.vector.tensor_tensor(bsum[:, :], bsum[:, :], gs0[:, :, 0], ALU.add).then_inc(s_br, 1)
                elif what == "fold":
                    m = ps_m[c % 2]
                    if c >= KT:
                        dve.wait_ge(s_f, NF * i + c + 1)
                        kt = c - KT
                        d = m[:, kt * P:(kt + 1) * P]
                        nc.vector.scalar_tensor_tensor(d, ident, sd0[:, kt:kt + 1], d, ALU.mult,
                                                       ALU.add).then_inc(s_fd, 1)
                    dve.wait_ge(s_fh, NF * i + c + 1)
                    nc.vector.scalar_tensor_tensor(w16[:, c, 1, :], m[:, 0:C], r64[:, c % KT:c % KT + 1],
                                                   w16[:, c, 0, :], ALU.mult, ALU.subtract).then_inc(s_fl, 1)
                elif what == "keep":
                    m = KT * c + n
                    if c == 0:
                        dve.wait_ge(s_mm, GM * i + m + 1)
                        wait(dve, s_me, GM * i)
                        dve.wait_ge(s_br, i + 1)
                        nc.vector.tensor_scalar(yb[:, n:n + 1], ps_m[m % 2][:, 0:1], -1.0 / WS, bsum[:, n:n + 1],
                                                ALU.mult, ALU.add).then_inc(s_yb, 1)
                    dve.wait_ge(s_me, GM * i + m + 1)
                    nc.vector.bn_stats(st1[:, n, c, :], x1_rows(n, c)).then_inc(s_st1, 1)
                elif what == "moments1":
                    j = i - 1
                    step = Steps(dve, s_c1, XG1, j)
                    dve.wait_ge(s_st1, GM * (j + 1))
                    nc.vector.memset(tmp1[:, :], 0.0)
                    moments(step, st1, mv1, tmp1)
                    step.then(nc.vector.tensor_tensor(mv1[:, :, 1], mv1[:, :, 1], tmp1[:, :], ALU.add))
                    in_parts(step, mv1, tmp1, mp1).then_inc(s_m1, 1)
                    chains["x1"] = step
                elif what == "norm1":
                    j = i - 1
                    step = chains["x1"]
                    dve.wait_ge(s_g1, j + 1)
                    joined(step, gs1, stat1_ps)
                    step.then(nc.vector.tensor_tensor(var1[:, :], gs1[:, :, 0], gs1[:, :, 0], ALU.mult))
                    step.then(nc.vector.tensor_tensor(var1[:, :], gs1[:, :, 1], var1[:, :], ALU.subtract))
                    nc.vector.tensor_scalar(var1[:, :], var1[:, :], 0.0, EPS, ALU.max, ALU.add).then_inc(s_v1, 1)
                    dve.wait_ge(s_r1, j + 1)
                    newton(step, var1, rs1, tmp1)
                    step.then(nc.vector.tensor_tensor(nb1[:, :], gs1[:, :, 0], rs1[:, :], ALU.mult))
                    step(nc.vector.tensor_scalar(nb1[:, :], nb1[:, :], -1.0, None, ALU.mult))
                    step.settle()
                    step.end()
                elif what == "sums":
                    j = i - 1
                    done = CT * j + c
                    wait(dve, s_s, done)
                    wait(dve, s_q, done)
                    for kt in range(KT):
                        nc.vector.tensor_scalar(padded(xg)[:, 2 * kt:2 * kt + 2, :], x1_slab(kt, c),
                                                rs1[:, kt:kt + 1], nb1[:, kt:kt + 1], ALU.mult,
                                                ALU.add).then_inc(s_xg, 1)
                    dve.wait_ge(s_xg, KT * (done + 1))
                    wait(dve, s_lo, 2 * (CT * j + max(0, c - 1)))
                    nc.vector.tensor_tensor_scan(rsum[:, c % 2, :], xg[:, LEAD:LEAD + SLAB], xg[:, 0:SLAB],
                                                 0.0, ALU.add, ALU.subtract).then_inc(s_s, 1)
                elif what == "square_sums":
                    dve.wait_ge(s_q, CT * (i - 1) + c + 1)
                    nc.vector.tensor_tensor_scan(qsum[:, c % 2, :], xq[:, LEAD:LEAD + SLAB], xq[:, 0:SLAB],
                                                 0.0, ALU.add, ALU.subtract).then_inc(s_qw, 1)
                elif what == "finish":
                    j, n = i - 1, c % TILES
                    done = CT * j + c
                    dve.wait_ge(s_num, done + 1)
                    dve.wait_ge(s_rec, done + 1)
                    wait(dve, s_st[n], 2 * 16 * (CHUNKS * j + c // TILES))
                    nc.vector.scalar_tensor_tensor(outb[:, n, :], ps_num[n % 2][0:OPX, 0:C], TINY,
                                                   rec[:, n % 2, :], ALU.add, ALU.mult).then_inc(s_rat, 1)
                    dve.wait_ge(s_xp, done + 1)
                    dve.wait_ge(s_rat, done + 1)
                    nc.vector.tensor_tensor(outb[:, n, :], ps_x1[n % 2][0:OPX, 0:C], outb[:, n, :],
                                            ALU.add).then_inc(s_out, 1)

            rounds(dve, do)

        @block.tensor
        def _(pe):
            pe.wait_ge(s_const, 32)
            pe.wait_ge(s_w, 16 * 10)
            for n in range(2 * KT):
                src = (wA, wB)[n // KT]
                wait(pe, s_sTc, n - 1)
                for t in range(KT):
                    last = nc.tensor.transpose(ps_m[n % 2][:, t * P:(t + 1) * P],
                                               src[:, t, (n % KT) * P:(n % KT + 1) * P], ident)
                last.then_inc(s_sT, 1)
            pe.wait_ge(s_sTc, 2 * KT)
            for n in range(2 * KT):
                src = (whT, wcT)[n // KT]
                wait(pe, s_sRc, n - 1 + 2)
                for t in range(KT):
                    last = nc.tensor.matmul(ps_num[n % 2][:, 0:CQ], src[:, t, (n % KT) * P:(n % KT + 1) * P],
                                            wr1[:, t, :], start=(t == 0), stop=(t == KT - 1))
                last.then_inc(s_sR, 1)
            pe.wait_ge(s_sRc, 2)
            for t in range(KT):
                last = nc.tensor.matmul(ps_x1[0][0:CQ, 0:1], wr1[:, t, :], tmp0[:, t:t + 1],
                                        start=(t == 0), stop=(t == KT - 1))
            last.then_inc(s_sR, 1)
            pe.wait_ge(s_sRc, 2 * KT + 4)

            def group_moments(dst, mp):
                for m in range(KT):
                    near = [t for t in range(KT) if abs(t - m) <= 1]
                    for t in near:
                        last = nc.tensor.matmul(dst[:, m, :], k16(f"group{t}{m}"),
                                                mp[:, t, :, :].rearrange("p k s -> p (k s)"),
                                                start=(t == near[0]), stop=(t == near[-1]))
                return last

            def do(it, i):
                what, c, n = it
                if what == "read":
                    img = i + 1
                    m = GM * img + KT * c + n
                    if n == 0:
                        slot = c % 2
                        per = (CHUNKS + 1 - slot) // 2
                        pe.wait_ge(s_x[slot], 16 * (per * img + c // 2 + 1))
                        if c == 0:
                            wait(pe, s_br, img)
                    wait(pe, s_pf, m)
                    for t in range(TILES):
                        last = nc.tensor.transpose(ps_p[:, t * TPX:(t + 1) * TPX],
                                                   xin[c % 2][:, t, n * P:(n + 1) * P], ident[0:TPX, 0:TPX])
                    last.then_inc(s_p, 1)
                elif what == "norm0":
                    pe.wait_ge(s_m0, i + 2)
                    pe.wait_ge(s_pf, GM * (i + 2))
                    group_moments(stat_ps, mp0).then_inc(s_g0, 1)
                elif what == "norm1":
                    pe.wait_ge(s_m1, i)
                    wait(pe, s_out, CT * (i - 1))
                    group_moments(stat1_ps, mp1).then_inc(s_g1, 1)
                elif what == "hidden":
                    pe.wait_ge(s_hx, i + 2)
                    for s, r in enumerate((r_h, r_c)):
                        for t in range(KT):
                            last = nc.tensor.matmul(h_ps, r[:, t, :], hx[:, s, t:t + 1],
                                                    start=(s == 0 and t == 0), stop=(s == 1 and t == KT - 1))
                    last.then_inc(s_h, 1)
                elif what == "gate":
                    pe.wait_ge(s_gel, i + 2)
                    for m in range(KT):
                        w = wr2[:, m * 3 * P:(m + 1) * 3 * P].rearrange("p (c s) -> p c s", s=3)
                        for s in range(3):
                            last = nc.tensor.matmul(a_ps[:, m, s:s + 1], w[:, :, s], gel[:, :],
                                                    start=True, stop=True)
                    last.then_inc(s_a, 1)
                elif what == "bias":
                    pe.wait_ge(s_ca, XA * (i + 2))
                    for m in range(KT):
                        for t in range(KT):
                            last = nc.tensor.matmul(b_ps[:, m:m + 1], wp[:, t, m * P:(m + 1) * P], u[:, t:t + 1],
                                                    start=(t == 0), stop=(t == KT - 1))
                    last.then_inc(s_b, 1)
                elif what == "fold":
                    pe.wait_ge(s_wA, 2 * KT * i + (KT if c < KT else 2 * KT))
                    if c < 2:
                        wait(pe, s_me, GM * i)
                    else:
                        pe.wait_ge(s_fl, NF * i + c - 1)
                    left, right = (whT, wA) if c < KT else (wcT, wB)
                    for t in range(KT):
                        last = nc.tensor.matmul(ps_m[c % 2][:, 0:C], left[:, t, (c % KT) * P:(c % KT + 1) * P],
                                                right[:, t, :], start=(t == 0), stop=(t == KT - 1))
                    last.then_inc(s_f, 1)
                elif what == "project":
                    m = KT * c + n
                    if m < 2:
                        pe.wait_ge(s_fl, NF * (i + 1))
                    else:
                        pe.wait_ge(s_me, GM * i + m - 1)
                    if n == 0:
                        nth = sum(1 for e in range(c) if SLOT[e] == SLOT[c])
                        pe.wait_ge(s_sh[SLOT[c]], 16 * NRES * (USES[SLOT[c]] * i + nth + 1))
                        if c == 0:
                            pe.wait_ge(s_pad, i + 1)
                    e = 1 if c == 0 else 0
                    a = HALO + c * CPX
                    terms = [(f, wpart, xpart) for f in range(NF) for wpart, xpart in ((0, 0), (1, 0), (0, 1))]
                    for t, (f, wpart, xpart) in enumerate(terms):
                        kt = f % KT
                        rhs = (sh[:, SLOT[c], kt, xpart, 2 - e:2 + CPX] if f < KT
                               else hl[:, kt, xpart, a - e:a + CPX])
                        last = nc.tensor.matmul(ps_m[m % 2][:, 0:CPX + e], w16[:, f, wpart, n * P:(n + 1) * P],
                                                rhs, start=(t == 0), stop=(t == len(terms) - 1))
                    last.then_inc(s_mm, 1)
                elif what == "tile":
                    j, n = i - 1, c % TILES
                    done = CT * j + c
                    pe.wait_ge(s_lo, 2 * (done + 1))
                    for src, dst, ready in ((qsp, ps_den, s_den), (rsp, ps_num[n % 2], s_num)):
                        if dst is ps_den:
                            wait(pe, s_ln, done)
                        else:
                            wait(pe, s_rat, CT * j + max(0, c - 1))
                        for t, (lo, hi) in enumerate(BANDS):
                            a = 2 * t * PITCH + 2
                            for part in range(2):
                                last = nc.tensor.matmul(dst[0:OPX, lo:hi], src[:, c % AHEAD, part, a:a + OPX],
                                                        k16(f"band{t}"), start=(t == 0 and part == 0),
                                                        stop=(t == KT - 1 and part == 1), skip_group_check=True)
                        last.then_inc(ready, 1)
                    wait(pe, s_out, CT * j + max(0, c - 1))
                    if c == 0:
                        pe.wait_ge(s_v1, j + 1)
                    a = 2 * c * PITCH
                    for t in range(KT):
                        last = nc.tensor.transpose(ps_x1[n % 2][0:OPX, t * P:(t + 1) * P], x1T[:, t, a:a + OPX],
                                                   ident)
                    last.then_inc(s_xp, 1)

            rounds(pe, do)


def kernel(x, L0_conv_w_h, L0_conv_b_h, L0_conv_w_c, L0_conv_b_c, L0_conv_w_r1, L0_conv_b_r1, L0_conv_w_r2,
           L0_conv_b_r2, L0_conv_w_p, L0_conv_b_p):
    import concourse.bacc as bacc
    from concourse.bass_utils import run_bass_kernel_spmd

    g = geometry(x.shape)
    (blob, ones), at = constant_blob(g)
    nc = bacc.Bacc("TRN2", target_bir_lowering=False, num_devices=1)
    given = dict(x=x, w_h=L0_conv_w_h, b_h=L0_conv_b_h, w_c=L0_conv_w_c, b_c=L0_conv_b_c, w_r1=L0_conv_w_r1,
                 b_r1=L0_conv_b_r1, w_r2=L0_conv_w_r2, b_r2=L0_conv_b_r2, w_p=L0_conv_w_p, b_p=L0_conv_b_p,
                 blob=blob, ones=ones)
    arrays, args = {}, {}
    for name, a in given.items():
        a = np.ascontiguousarray(a)
        arrays[f"in_{name}"] = a
        args[name] = nc.dram_tensor(f"in_{name}", a.shape, mybir.dt.from_np(a.dtype), kind="ExternalInput").ap()
    args["out"] = nc.dram_tensor("out_x", x.shape, mybir.dt.float32, kind="ExternalOutput").ap()
    build(nc, g, at, **args)
    return run_bass_kernel_spmd(nc, [arrays], core_ids=[0]).results[0]["out_x"]
```

```python
import numpy as np
import concourse.bass as bass
from concourse import mybir
from contextlib import ExitStack

WINDOW_W, WINDOW_C = 5, 20
SHIFT_PERIOD = 8
SHIFTS = (-2, -1, 0, 1, 2, 1, 0, -1)
GROUPS = 32
EPS = 1e-5
TINY = 2.0 ** -63
P = 128

ERF_TOP = (-2.72614225801306e-10, 2.77068142495902e-08, -2.10102402082508e-06, -5.69250639462346e-05,
           -7.34990630326855e-04, -2.95459980854025e-03, -1.60960333262415e-02)
ERF_LOW = (0.0, 0.0, -1.45660718464996e-05, -2.13374055278905e-04, -1.68282697438203e-03,
           -7.37332916720468e-03, -1.42647390514189e-02)


def geometry(shape):
    B, H, W, C = shape
    g = dict(B=B, H=H, W=W, C=C, KT=C // P, NPX=H * W, ROWS=8, TPX=2 * W)
    g["PITCH"] = W + 2
    g["OPX"] = 2 * g["PITCH"] - 2
    g["CHUNKS"] = H // g["ROWS"]
    g["CPX"] = g["ROWS"] * W
    g["TILES"] = g["CPX"] // g["TPX"]
    return g


def bands(C):
    lo, hi = WINDOW_C // 2, WINDOW_C - WINDOW_C // 2 - 1
    return [(max(0, k - hi), min(C, k + P + lo)) for k in range(0, C, P)]


def constant_blob(g):
    C, KT, W, H = g["C"], g["KT"], g["W"], g["H"]
    lo, hi = WINDOW_C // 2, WINDOW_C - WINDOW_C // 2 - 1
    blobs, at = ([], []), {}

    def put(name, a, blob=0):
        full = np.zeros((P, a.shape[1]), np.float32)
        full[:a.shape[0]] = a
        n = sum(b.shape[1] for b in blobs[blob])
        blobs[blob].append(full)
        at[name] = (n, n + a.shape[1])

    put("ident", np.eye(P))
    c = np.arange(C)
    per = C // GROUPS
    same = (c[:, None] // per == c[None, :] // per).astype(np.float64)
    for k in range(KT):
        for m in range(KT):
            if abs(k - m) <= 1:
                put(f"group{k}{m}", same[k * P:(k + 1) * P, m * P:(m + 1) * P], 1)
    box = ((c[:, None] >= c[None, :] - lo) & (c[:, None] <= c[None, :] + hi)).astype(np.float64)
    for k, (a, b) in enumerate(bands(C)):
        put(f"band{k}", box[k * P:(k + 1) * P, a:b], 1)
    w = np.minimum(np.arange(g["OPX"]) % g["PITCH"], W - 1)
    taps = np.minimum(w + WINDOW_W // 2, W - 1) - np.maximum(w - WINDOW_W // 2, 0) + 1
    put("taps", taps[:, None])
    s = np.array(SHIFTS)[np.arange(P) % SHIFT_PERIOD]
    lost = np.stack([s <= -1, s <= -2, s >= 2, s >= 1], 1).astype(np.float64)
    put("lost", lost / (H * W))
    put("lost_share", (lost.sum(1) / H)[:, None])
    put("erf", np.repeat(np.stack([ERF_TOP, ERF_LOW], 1).reshape(1, -1), P, 0))
    return [np.ascontiguousarray(np.concatenate(b, 1)) for b in blobs], at


class Steps:

    def __init__(self, eng, sem, per_image, image):
        self.eng, self.sem, self.per, self.base, self.k = eng, sem, per_image, per_image * image, 0

    def __call__(self, ins):
        self.k += 1
        ins.then_inc(self.sem, 1)

    def settle(self):
        self.eng.wait_ge(self.sem, self.base + self.k)

    def then(self, ins):
        self(ins)
        self.settle()

    def end(self):
        assert self.k == self.per, (self.k, self.per)


def build(nc, g, at, x, w_h, b_h, w_c, b_c, w_r1, b_r1, w_r2, b_r2, w_p, b_p, blob, ones, out):
    f32, f16, bf16 = mybir.dt.float32, mybir.dt.float16, mybir.dt.bfloat16
    ALU, ACT, AX = mybir.AluOpType, mybir.ActivationFunctionType, mybir.AxisListType
    B, H, W, C, KT, NPX = (g[k] for k in ("B", "H", "W", "C", "KT", "NPX"))
    ROWS, TPX, CHUNKS, CPX, TILES = (g[k] for k in ("ROWS", "TPX", "CHUNKS", "CPX", "TILES"))
    CQ = w_r1.shape[1]
    BANDS = bands(C)
    BANK = 512
    HALO = 2 * W
    PITCH, OPX = g["PITCH"], g["OPX"]
    SR = KT * 2
    SLAB = SR * PITCH
    LEAD = 5
    WS = 64.0
    GM = KT * CHUNKS
    CT = CHUNKS * TILES
    NF = 2 * KT
    SLOT = (0, 1, 2, 0, 1, 2, 3)
    SLOTS = 4
    USES = [SLOT.count(s) for s in range(SLOTS)]
    NRES = SHIFT_PERIOD
    XG0, XG1, XH, XA = 23, 18, 15, 11
    READS = (6, 5, 4, 0, 1, 2, 3)
    BY_DVE = 4
    AHEAD = 4
    STAGED = (4, 5, 6)

    x_v = x.rearrange("b h w c -> (b h w) c").rearrange("(n t p) c -> n p t c", p=TPX, t=TILES)
    out_v = out.rearrange("b (n t r) w c -> b n t r w c", r=2, t=TILES)

    ctx = ExitStack()
    with ctx:
        def sb(name, shape, dt=f32):
            return ctx.enter_context(nc.sbuf_tensor(name, shape, dt))

        def sem(name):
            return ctx.enter_context(nc.semaphore(name))

        cst = sb("cst", [P, blob.shape[1]])
        whT = sb("whT", [P, KT, C])
        wcT = sb("wcT", [P, KT, C])
        wp16 = sb("wp16", [P, KT, 2, C], f16)
        wr16 = sb("wr16", [CQ, 2, KT * P * 3], f16)
        wp = sb("wp", [P, KT, C])
        wA = sb("wA", [P, KT, C])
        wB = sb("wB", [P, KT, C])
        r_h = sb("r_h", [P, KT, CQ])
        r_c = sb("r_c", [P, KT, CQ])
        cols = sb("cols", [P, 3, KT])
        br1 = sb("br1", [CQ, 1])
        br2 = sb("br2", [P, KT, 3])
        hconst = sb("hconst", [CQ, 1])
        w16 = sb("w16", [P, NF, 2, C], f16)
        xin = [sb(f"xin{s}", [TPX, TILES, C]) for s in range(2)]
        hl = sb("hl", [P, KT, 2, NPX + 2 * HALO], f16)
        sh = sb("sh", [P, SLOTS, KT, 2, CPX + 2], f16)
        x1T = sb("x1T", [P, KT, H * PITCH])
        stg = sb("stg", [P, len(STAGED), KT, 2, CPX], f16)
        xg = sb("xg", [P, 2, LEAD + SLAB + 3])
        xq = sb("xq", [P, LEAD + SLAB + 3])
        rsum = sb("rsum", [P, 2, SLAB])
        qsum = sb("qsum", [P, 2, SLAB])
        rsp = sb("rsp", [P, AHEAD, 2, SLAB], bf16)
        qsp = sb("qsp", [P, AHEAD, 2, SLAB], bf16)
        rec = sb("rec", [OPX, 2, C])
        outb = sb("outb", [OPX, TILES, C])
        st0 = sb("st0", [P, KT, CHUNKS, 6])
        st1 = sb("st1", [P, KT, CHUNKS, 6])
        mv0 = sb("mv0", [P, KT, 2])
        mv1 = sb("mv1", [P, KT, 2])
        mp0 = sb("mp0", [P, KT, 3, 2], bf16)
        mp1 = sb("mp1", [P, KT, 3, 2], bf16)
        one16 = sb("one16", [P, ones.shape[1]], bf16)
        gs0 = sb("gs0", [P, KT, 2])
        gs1 = sb("gs1", [P, KT, 2])
        tmp0 = sb("tmp0", [P, KT])
        tmp1 = sb("tmp1", [P, KT])
        var0 = sb("var0", [P, KT])
        var1 = sb("var1", [P, KT])
        rs0 = sb("rs0", [P, KT])
        rs1 = sb("rs1", [P, KT])
        lnv0 = sb("lnv0", [P, KT])
        lnv1 = sb("lnv1", [P, KT])
        nb1 = sb("nb1", [P, KT])
        sd0 = sb("sd0", [P, KT])
        rowp = sb("rowp", [P, KT, 2, 2, 2])
        rows = sb("rows", [P, KT, 4])
        hx = sb("hx", [P, 2, KT])
        padv = sb("padv", [P, KT, 2], f16)
        hp = sb("hp", [CQ, 8])
        ef = sb("ef", [CQ, 2])
        gel = sb("gel", [CQ, 1])
        gel16 = sb("gel16", [CQ, 2], f16)
        al = sb("al", [P, KT, 3])
        mx = sb("mx", [P, KT])
        sm = sb("sm", [P, KT])
        gA = sb("gA", [P, KT])
        gB = sb("gB", [P, KT])
        u = sb("u", [P, KT])
        u2 = sb("u2", [P, KT])
        u16 = sb("u16", [P, KT, 2], f16)
        bsum = sb("bsum", [P, KT])
        yb = sb("yb", [P, KT])
        lost = sb("lost", [P, KT])
        tinyc = sb("tinyc", [P, 1])
        mark = sb("mark", [P, 2])

        ps_m = [ctx.enter_context(nc.psum_tensor(f"ps_m{s}", [P, BANK], f32)) for s in range(2)]
        ps_num = [ctx.enter_context(nc.psum_tensor(f"ps_num{s}", [P, BANK], f32)) for s in range(2)]
        ps_den = ctx.enter_context(nc.psum_tensor("ps_den", [P, BANK], f32))
        ps_x1 = [ctx.enter_context(nc.psum_tensor(f"ps_x1{s}", [P, BANK], f32)) for s in range(2)]
        ps_p = ctx.enter_context(nc.psum_tensor("ps_p", [P, BANK], f32))

        def lent(t, start, n, parts=P):
            return x1T[0:parts, t, start:start + n]

        def by_tile(a):
            return a.rearrange("p (t n) -> p t n", t=KT)

        wh_in, wc_in = (by_tile(lent(0, n * KT * C, KT * C)) for n in range(2))
        wr1 = by_tile(lent(0, 2 * KT * C, KT * CQ))
        wr2 = lent(2, 0, KT * P * 3, CQ)
        ones32 = lent(2, KT * P * 3, ones.shape[1])

        def k(name, parts=P):
            a, b = at[name]
            return cst[0:parts, a:b]

        def k16(name):
            a, b = at[name]
            return one16[:, a:b]

        ident = k("ident")
        stat_ps = ps_p[:, 0:6 * KT].rearrange("p (m s) -> p m s", s=6)
        h_ps = ps_p[0:CQ, 24:25]
        a_ps = ps_p[:, 32:32 + 6 * KT].rearrange("p (m s k) -> p m s k", s=3, k=2)
        b_ps = ps_p[:, 64:64 + 2 * KT].rearrange("p (m k) -> p m k", k=2)
        stat1_ps = ps_x1[0][:, 0:6 * KT].rearrange("p (m s) -> p m s", s=6)

        def padded(t):
            return t[:, LEAD - 2:LEAD - 2 + SLAB].rearrange("p (r w) -> p r w", w=PITCH)[:, :, 2:PITCH]

        def x_chunk(c, kt, part):
            if c in STAGED:
                return stg[:, STAGED.index(c), kt, part, :]
            return hl[:, kt, part, HALO + c * CPX:HALO + (c + 1) * CPX]

        def x1_rows(kt, c):
            a = c * ROWS * PITCH
            return x1T[:, kt, a:a + ROWS * PITCH].rearrange("p (r w) -> p r w", w=PITCH)[:, :, 0:W]

        def x1_slab(kt, s):
            a = 2 * s * PITCH
            return x1T[:, kt, a:a + 2 * PITCH].rearrange("p (r w) -> p r w", w=PITCH)[:, :, 0:W]

        s_const = sem("const_loaded")
        s_w = sem("weights_loaded")
        s_zero = sem("zeros_written")
        s_sT = sem("setup_transposed")
        s_sTc = sem("setup_copied")
        s_sR = sem("setup_products")
        s_sRc = sem("setup_products_copied")
        s_whi = sem("weights_high_written")
        s_wlo = sem("weights_low_written")
        s_gap = sem("gaps_written")
        s_x = [sem(f"x_loaded{s}") for s in range(2)]
        s_p = sem("x_transposed")
        s_hi = sem("x_high_written")
        s_pf = sem("x_low_and_stats_written")
        s_sh = [sem(f"shifted_loaded{s}") for s in range(SLOTS)]
        s_pad = sem("pads_written")
        s_c0 = sem("x_stat_steps")
        s_c1 = sem("x1_stat_steps")
        s_ch = sem("gelu_steps")
        s_ca = sem("softmax_steps")
        s_erf = sem("erf_steps")
        s_bs = sem("bias_steps")
        s_m0 = sem("x_moments")
        s_m1 = sem("x1_moments")
        s_g0 = sem("x_group_moments")
        s_g1 = sem("x1_group_moments")
        s_v0 = sem("x_variance")
        s_v1 = sem("x1_variance")
        s_l0 = sem("x_log")
        s_l1 = sem("x1_log")
        s_r0 = sem("x_rstd_first")
        s_r1 = sem("x1_rstd_first")
        s_hx = sem("means_ready")
        s_h = sem("hidden_product")
        s_gel = sem("gelu_ready")
        s_a = sem("logits")
        s_am = sem("logits_less_max")
        s_ae = sem("exponentials")
        s_g = sem("gates_ready")
        s_wA = sem("gated_weights")
        s_b = sem("bias_product")
        s_br = sem("bias_read")
        s_f = sem("fold_product")
        s_fd = sem("fold_diagonal")
        s_fh = sem("fold_high")
        s_fl = sem("fold_low")
        s_mm = sem("projected")
        s_yb = sem("bias_ready")
        s_me = sem("x1_written")
        s_st1 = sem("x1_stats_written")
        s_n1 = sem("norm1_ready")
        s_xg = sem("xg_written")
        s_s = sem("row_sums_written")
        s_q = sem("squares_written")
        s_qw = sem("square_sums_written")
        s_sh_hi = sem("sums_high_written")
        s_lo = sem("sums_low_written")
        s_stc = sem("staged_copied")
        s_den = sem("den_ready")
        s_num = sem("num_ready")
        s_xp = sem("x1_back")
        s_ln = sem("log_written")
        s_rec = sem("reciprocal_written")
        s_rat = sem("ratio_written")
        s_out = sem("out_written")
        s_st = [sem(f"out_stored{t}") for t in range(TILES)]

        def wait(eng, s, value):
            if isinstance(value, int) and value <= 0:
                return
            eng.wait_ge(s, value)

        ORDER = (
            "moments1 fold:0 norm1 fold:1 normalise:0 sums:0 square_sums:0 fold:2 fold:3 normalise:1 "
            "sums:1 split:0 square_sums:1 normalise:2 fold:4 sums:2 square_sums:2 normalise:3 split:1 "
            "fold:5 sums:3 square_sums:3 normalise:4 split:2 tile:0 tile:1 read tile:2 project:0 read "
            "tile:3 keep:0 project:1 read",
            "tile:0 project_before read tile:1 read tile:2 project:0 read tile:3 keep:0 project:1 read",
            "tile:0 read project_before tile:1 read tile:2 project:0 read tile:3 keep:0 project:1 read",
            "tile:0 read project_before tile:1 read project:0 tile:2 read tile:3 keep:0 project:1 read",
            "tile:0 project_before tile:1 read tile:2 project:0 read tile:3 keep:0 project:1 read lost",
            "tile:0 project_before tile:1 read project:0 tile:2 read tile:3 keep:0 project:1 read "
            "moments0",
            "tile:0 project_before tile:1 norm0 project:0 tile:2 hidden tile:3 keep:0 project:1 keep:1 "
            "gate project:2 keep:2 bias",
        )
        SECOND = ("moments1", "norm1", "normalise", "sums", "square_sums", "split")
        NEXT = ("lost", "moments0", "norm0", "hidden", "gate", "bias")

        def items(c_too, m_too, p_too):
            reads = iter([("read", r, n) for r in range(CHUNKS) for n in range(KT)])

            def slab(what, s):
                if c_too and s < CT:
                    yield what, s, 0

            def tile(c, t):
                s = TILES * c + t
                yield from slab("normalise", s + AHEAD + 1)
                yield from slab("sums", s + AHEAD)
                if m_too and c and t < KT - 1:
                    yield "keep", c - 1, t + 1
                yield from slab("tile", s)
                yield from slab("finish", s)
                yield from slab("square_sums", s + AHEAD)
                yield from slab("split", s + AHEAD - 1)

            for c, work in enumerate(ORDER):
                for word in work.split():
                    what, _, n = word.partition(":")
                    if what == "tile":
                        yield from tile(c, int(n))
                    elif what in SECOND:
                        yield from slab(what, int(n or 0))
                    elif what == "fold" and m_too:
                        yield what, int(n), 0
                    elif what in ("project", "keep") and m_too:
                        yield what, c, int(n)
                    elif what == "project_before" and m_too and c:
                        yield "project", c - 1, KT - 1
                    elif what == "read" and p_too:
                        yield next(reads)
                    elif what in NEXT and p_too:
                        yield what, 0, 0

        def rounds(eng, do):
            for r in range(CHUNKS):
                for n in range(KT):
                    do(("read", r, n), -1)
            for what in ("lost", "moments0", "norm0", "hidden", "gate", "bias"):
                do((what, 0, 0), -1)
            for it in items(False, True, True):
                do(it, 0)
            for it in items(True, True, True):
                do(it, 1)
            with eng.Fori(2, B - 1) as i:
                for it in items(True, True, True):
                    do(it, i)
            for it in items(True, True, False):
                do(it, B - 1)
            for it in items(True, False, False):
                do(it, B)

        def normalise(eng, s):
            for kt in range(KT):
                eng.tensor_scalar(padded(xg[:, s % 2, :])[:, 2 * kt:2 * kt + 2, :], x1_slab(kt, s),
                                  rs1[:, kt:kt + 1], nb1[:, kt:kt + 1], ALU.mult, ALU.add).then_inc(s_xg, 1)

        def read_bank(i, m):
            return ps_m[1] if isinstance(i, int) and i < 0 and m % 2 else ps_p

        PARTED = [(wp[:, :, :], wp16[:, :, 0, :], wp16[:, :, 1, :]),
                  (wr2, wr16[:, 0, :], wr16[:, 1, :])]

        block = ctx.enter_context(nc.Block())

        @block.sync
        def _(sp):
            sp.dma_start(cst[:, :], blob).then_inc(s_const, 16)
            sp.dma_start(ones32, ones).then_inc(s_const, 16)
            for dst, src in ((wh_in, w_h), (wc_in, w_c), (wp, w_p)):
                sp.dma_start(dst[:, :, :], src.rearrange("(t p) n -> p t n", p=P)).then_inc(s_w, 16)
            sp.dma_start(wr1[:, :, :], w_r1.rearrange("(t p) n -> p t n", p=P)).then_inc(s_w, 16)
            sp.dma_start(wr2, w_r2).then_inc(s_w, 16)
            for n, b in enumerate((b_h, b_c, b_p)):
                sp.dma_start(cols[:, n, :], b.rearrange("(t p) -> p t", p=P),
                             allow_slow_non_contiguous=True).then_inc(s_w, 16)
            sp.dma_start(br1[:, :], b_r1.rearrange("(p o) -> p o", o=1),
                         allow_slow_non_contiguous=True).then_inc(s_w, 16)
            sp.dma_start(br2[:, :, :], b_r2.rearrange("(t p s) -> p t s", p=P, s=3)).then_inc(s_w, 16)
            for c in range(2):
                sp.dma_start(xin[c][:, :, :], x_v[READS[c]]).then_inc(s_x[c], 16)

            def shift(i, c):
                prev = [d for d in range(c) if SLOT[d] == SLOT[c]]
                if prev:
                    wait(sp, s_mm, GM * i + KT * (prev[-1] + 1))
                for r in range(NRES):
                    a = HALO + c * CPX - SHIFTS[r] * W
                    sp.dma_start(sh[r:P:NRES, SLOT[c], :, :, 2:2 + CPX],
                                 hl[r:P:NRES, :, :, a:a + CPX]).then_inc(s_sh[SLOT[c]], 16)

            def do(it, i):
                what, c, n = it
                if what == "fold" and c == 0:
                    wait(sp, s_mm, GM * i)
                    for n, d in enumerate(STAGED):
                        a = HALO + d * CPX
                        sp.dma_start(hl[:, :, :, a:a + CPX], stg[:, n, :, :, :]).then_inc(s_stc, 16)
                    shift(i, 1)
                    shift(i, 2)
                    if not isinstance(i, int) or i < B - 1:
                        for r in range(2):
                            sp.dma_start(xin[r][:, :, :], x_v[CHUNKS * i + (CHUNKS + READS[r])]).then_inc(s_x[r], 16)
                    sp.wait_ge(s_stc, 16 * len(STAGED) * (i + 1))
                    shift(i, 6)
                elif what == "hidden":
                    sp.wait_ge(s_pad, i + 2)
                    shift(i + 1, 0)
                elif what == "project" and n == KT - 1 and c < 3:
                    shift(i, c + 3)
                elif what == "read" and n == KT - 1 and c + 2 < CHUNKS:
                    sp.wait_ge(s_p, GM * (i + 1) + KT * (c + 1))
                    sp.dma_start(xin[c % 2][:, :, :],
                                 x_v[CHUNKS * i + (CHUNKS + READS[c + 2])]).then_inc(s_x[c % 2], 16)
                elif what == "finish":
                    j, n = i - 1, c % TILES
                    sp.wait_ge(s_out, CT * j + c + 1)
                    for r in range(2):
                        sp.dma_start(out_v[j, c // TILES, n, r],
                                     outb[r * PITCH:r * PITCH + W, n, :]).then_inc(s_st[n], 16)

            rounds(sp, do)
            for t in range(TILES):
                sp.wait_ge(s_st[t], 2 * 16 * CHUNKS * B)

        @block.gpsimd
        def _(pool):
            nc.gpsimd.memset(xg[:, :, :], 0.0).then_inc(s_zero, 1)
            nc.gpsimd.memset(xq[:, :], 0.0).then_inc(s_zero, 1)
            nc.gpsimd.memset(tinyc[:, :], TINY).then_inc(s_zero, 1)
            pool.wait_ge(s_wlo, len(PARTED))
            pool.wait_ge(s_sRc, 2 * KT + 4)
            gaps = x1T[:, :, :].rearrange("p t (h w) -> p (t h) w", w=PITCH)[:, :, W:PITCH]
            nc.gpsimd.memset(gaps, 0.0).then_inc(s_gap, 1)

            def do(it, i):
                what, c, n = it
                if what == "normalise" and c >= BY_DVE:
                    j = i - 1
                    pool.wait_ge(s_c1, XG1 * (j + 1))
                    wait(pool, s_xg, KT * (CT * j + c))
                    wait(pool, s_s, CT * j + max(0, c - 1))
                    wait(pool, s_q, CT * j + max(0, c - 1))
                    nc.gpsimd.tensor_tensor(mark[:, 0:1], tinyc[:, :], tinyc[:, :], ALU.mult)
                    normalise(nc.gpsimd, c)
                elif what == "split":
                    done = CT * (i - 1) + c
                    for h, (src, dst) in enumerate(((qsum, qsp), (rsum, rsp))):
                        pool.wait_ge(s_sh_hi, 3 * done + (1, 3)[h])
                        r = c % AHEAD
                        nc.gpsimd.tensor_tensor(dst[:, r, 1, :], src[:, c % 2, :], dst[:, r, 0, :],
                                                ALU.subtract).then_inc(s_lo, 1)
                elif what == "norm0":
                    g = i + 1
                    pool.wait_ge(s_v0, g + 1)
                    if not (isinstance(i, int) and i < 0):
                        pool.wait_ge(s_mm, GM * i + KT)
                        for s in range(SLOTS):
                            pool.wait_ge(s_sh[s], 16 * NRES * USES[s] * g)
                    wait(pool, s_pad, g)
                    nc.gpsimd.tensor_tensor(mark[:, 1:2], tinyc[:, :], tinyc[:, :], ALU.mult)
                    for kt in range(KT):
                        for a in (0, HALO + NPX):
                            nc.gpsimd.tensor_copy(hl[:, kt, :, a:a + HALO],
                                                  padv[:, kt, :].unsqueeze(2).to_broadcast([P, 2, HALO]))
                    nc.gpsimd.tensor_copy(sh[:, 0, :, :, 1:2],
                                          padv[:, :, :].unsqueeze(3)).then_inc(s_pad, 1)
                elif what == "gate":
                    pool.wait_ge(s_g, i + 2)
                    wait(pool, s_f, NF * (i + 1))
                    for gate, dst in ((gA, wA), (gB, wB)):
                        for kt in range(KT):
                            nc.gpsimd.tensor_tensor(dst[:, kt, :], wp[:, kt, :],
                                                    gate[:, kt:kt + 1].to_broadcast([P, C]),
                                                    ALU.mult).then_inc(s_wA, 1)

            rounds(pool, do)

        def free_shift(eng, i, c):
            if isinstance(i, int) and i < 0:
                return
            for d in ((0, c) if c == 1 else (c,)):
                if d < CHUNKS:
                    nth = sum(1 for e in range(d) if SLOT[e] == SLOT[d])
                    eng.wait_ge(s_sh[SLOT[d]], 16 * NRES * (USES[SLOT[d]] * i + nth + 1))

        def rstd_start(act, s_v, s_l, s_r, var, lnv, rs, i):
            act.wait_ge(s_v, i + 1)
            nc.scalar.activation(lnv[:, :], var[:, :], ACT.Ln).then_inc(s_l, 1)
            act.wait_ge(s_l, i + 1)
            nc.scalar.activation(rs[:, :], lnv[:, :], ACT.Exp, scale=-0.5).then_inc(s_r, 1)

        @block.scalar
        def _(act):
            nc.scalar.preload_act_table_set("natural_log_exp_and_others")
            act.wait_ge(s_zero, 3)
            for n in range(2 * KT):
                act.wait_ge(s_sT, n + 1)
                dst = (whT, wcT)[n // KT]
                nc.scalar.copy(dst[:, n % KT, :], ps_m[n % 2][:, 0:C]).then_inc(s_sTc, 1)
            act.wait_ge(s_w, 16 * 10)
            act.wait_ge(s_sTc, 2 * KT)
            for src, high, _ in PARTED:
                nc.scalar.activation(high, src, ACT.Copy, scale=WS).then_inc(s_whi, 1)
            act.wait_ge(s_gap, 1)

            def do(it, i):
                what, c, n = it
                if what == "norm0":
                    rstd_start(act, s_v0, s_l0, s_r0, var0, lnv0, rs0, i + 1)
                elif what == "norm1":
                    rstd_start(act, s_v1, s_l1, s_r1, var1, lnv1, rs1, i - 1)
                elif what == "gate":
                    act.wait_ge(s_am, i + 2)
                    nc.scalar.activation(al[:, :, :], al[:, :, :], ACT.Exp).then_inc(s_ae, 1)
                elif what == "fold":
                    if c < KT:
                        act.wait_ge(s_f, NF * i + c + 1)
                    else:
                        act.wait_ge(s_fd, KT * i + c - KT + 1)
                    nc.scalar.activation(w16[:, c, 0, :], ps_m[(c + 1) % 2][:, 0:C], ACT.Copy,
                                         scale=rs0[:, c % KT:c % KT + 1]).then_inc(s_fh, 1)
                elif what == "read":
                    img = i + 1
                    d = READS[c]
                    act.wait_ge(s_p, GM * img + KT * c + n + 1)
                    if n == 0:
                        if d in STAGED:
                            wait(act, s_stc, 16 * len(STAGED) * img)
                        else:
                            wait(act, s_mm, GM * i + KT * (d + 1))
                            free_shift(act, i, d + 1)
                    nc.scalar.copy(x_chunk(d, n, 0), read_bank(i, KT * c + n)[:, 0:CPX]).then_inc(s_hi, 1)
                elif what == "keep":
                    m = KT * c + n
                    act.wait_ge(s_mm, GM * i + m + 1)
                    if c == 0:
                        act.wait_ge(s_yb, KT * i + n + 1)
                    if n == 0:
                        wait(act, s_xg, KT * (CT * (i - 1) + TILES * (c + 1)))
                        wait(act, s_xp, CT * (i - 1) + TILES * (c + 1))
                    a = 1 if c == 0 else 0
                    nc.scalar.activation(x1_rows(n, c), ps_m[m % 2][:, a:a + CPX].rearrange("p (r w) -> p r w", w=W),
                                         ACT.Identity, bias=yb[:, n:n + 1], scale=1.0 / WS).then_inc(s_me, 1)
                elif what == "square_sums":
                    done = CT * (i - 1) + c
                    act.wait_ge(s_xg, KT * (done + 1))
                    wait(act, s_qw, done)
                    nc.scalar.activation(padded(xq), padded(xg[:, c % 2, :]), ACT.Square).then_inc(s_q, 1)
                elif what == "split":
                    done = CT * (i - 1) + c
                    r, e = c % AHEAD, c % 2
                    act.wait_ge(s_qw, done + 1)
                    wait(act, s_num, CT * (i - 1) + max(0, c - AHEAD + 1))
                    nc.scalar.copy(qsp[:, r, 0, :], qsum[:, e, :]).then_inc(s_sh_hi, 1)
                    nc.scalar.activation(rsp[:, r, 0, :], rsum[:, e, :], ACT.Square).then_inc(s_sh_hi, 1)
                    act.wait_ge(s_sh_hi, 3 * done + 2)
                    nc.scalar.activation(rsum[:, e, :], rsum[:, e, :], ACT.Square).then_inc(s_sh_hi, 1)
                elif what == "tile":
                    j, n = i - 1, c % TILES
                    done = CT * j + c
                    act.wait_ge(s_den, done + 1)
                    wait(act, s_rat, CT * j + max(0, c - 1))
                    r = rec[:, n % 2, :]
                    nc.scalar.activation(r, ps_den[0:OPX, 0:C], ACT.Ln, bias=tinyc[0:OPX, :],
                                         scale=k("taps", OPX)).then_inc(s_ln, 1)
                    act.wait_ge(s_ln, done + 1)
                    nc.scalar.activation(r, r, ACT.Exp, scale=-1.0).then_inc(s_rec, 1)

            rounds(act, do)

        def newton(step, var, rs, tmp):
            step.then(nc.vector.tensor_tensor(tmp[:, :], rs[:, :], rs[:, :], ALU.mult))
            step.then(nc.vector.tensor_tensor(tmp[:, :], tmp[:, :], var[:, :], ALU.mult))
            step.then(nc.vector.tensor_scalar(tmp[:, :], tmp[:, :], -0.5, 1.5, ALU.mult, ALU.add))
            step.then(nc.vector.tensor_tensor(rs[:, :], rs[:, :], tmp[:, :], ALU.mult))

        @block.vector
        def _(dve):
            dve.wait_ge(s_w, 16 * 10)
            dve.wait_ge(s_const, 32)
            nc.vector.tensor_scalar(tmp0[:, :], cols[:, 0, :], 2.0, None, ALU.mult).then_inc(s_sRc, 1)
            dve.wait_ge(s_sRc, 1)
            nc.vector.tensor_tensor(tmp0[:, :], tmp0[:, :], cols[:, 1, :], ALU.add).then_inc(s_sRc, 1)
            for n in range(2 * KT):
                dve.wait_ge(s_sR, n + 1)
                dst, f = ((r_h, 2.0), (r_c, 1.0))[n // KT]
                nc.vector.tensor_scalar(dst[:, n % KT, :], ps_num[n % 2][:, 0:CQ], f, None,
                                        ALU.mult).then_inc(s_sRc, 1)
            dve.wait_ge(s_sR, 2 * KT + 1)
            nc.vector.tensor_tensor(hconst[:, :], ps_x1[0][0:CQ, 0:1], br1[:, :], ALU.add).then_inc(s_sRc, 1)
            dve.wait_ge(s_sRc, 2 * KT + 3)
            dve.wait_ge(s_zero, 3)

            chains = {}

            for n, (src, high, low) in enumerate(PARTED):
                dve.wait_ge(s_whi, n + 1)
                nc.vector.scalar_tensor_tensor(low, src, WS, high, ALU.mult, ALU.subtract).then_inc(s_wlo, 1)
            nc.vector.tensor_copy(one16[:, :], ones32).then_inc(s_sRc, 1)

            def in_parts(step, mv, tmp, mp):
                step.then(nc.vector.tensor_copy(mp[:, :, 0, :], mv[:, :, :]))
                step.then(nc.vector.tensor_tensor(mv[:, :, :], mv[:, :, :], mp[:, :, 0, :], ALU.subtract))
                step.then(nc.vector.tensor_copy(mp[:, :, 1, :], mv[:, :, :]))
                return nc.vector.tensor_tensor(mp[:, :, 2, :], mv[:, :, :], mp[:, :, 1, :], ALU.subtract)

            def joined(step, gs, ps):
                step.then(nc.vector.tensor_reduce(gs[:, :, :], ps.rearrange("p m (k s) -> p m s k", s=2), AX.X,
                                                  ALU.add))
                step.then(nc.vector.tensor_scalar(gs[:, :, :], gs[:, :, :], GROUPS / C, None, ALU.mult))

            def moments(step, st, mv, tmp):
                for kt in range(KT):
                    step(nc.vector.bn_aggr(mv[:, kt, :], st[:, kt, :, :].rearrange("p c s -> p (c s)")))
                step.settle()
                step.then(nc.vector.tensor_tensor(tmp[:, :], mv[:, :, 0], mv[:, :, 0], ALU.mult))

            def do(it, i):
                what, c, n = it
                if what == "read":
                    img = i + 1
                    m = GM * img + KT * c + n
                    dve.wait_ge(s_hi, m + 1)
                    d = READS[c]
                    bank = read_bank(i, KT * c + n)
                    nc.vector.tensor_tensor(x_chunk(d, n, 1), bank[:, 0:CPX], x_chunk(d, n, 0), ALU.subtract)
                    nc.vector.bn_stats(st0[:, n, d, :], bank[:, 0:CPX]).then_inc(s_pf, 1)
                elif what == "lost":
                    g = i + 1
                    step = Steps(dve, s_c0, XG0, g)
                    chains["x"] = step
                    dve.wait_ge(s_pf, GM * g + KT * (READS.index(0) + 1))
                    nc.vector.memset(lost[:, :], 0.0)
                    for e in range(2):
                        for kt in range(KT):
                            src = (hl[:, kt, :, HALO:HALO + 2 * W] if e == 0
                                   else stg[:, STAGED.index(CHUNKS - 1), kt, :, CPX - 2 * W:CPX])
                            ins = nc.vector.tensor_reduce(
                                rowp[:, kt, :, e, :], src.rearrange("p s (r w) -> p s r w", w=W), AX.X, ALU.add)
                            if kt == KT - 1:
                                step(ins)
                    step.settle()
                    step.then(nc.vector.tensor_tensor(
                        rows[:, :, :], rowp[:, :, 0].rearrange("p t e r -> p t (e r)"),
                        rowp[:, :, 1].rearrange("p t e r -> p t (e r)"), ALU.add))
                    for kt in range(KT):
                        ins = nc.vector.tensor_tensor(rows[:, kt, :], rows[:, kt, :], k("lost"), ALU.mult)
                    step.then(ins)
                    step.then(nc.vector.tensor_reduce(lost[:, :], rows[:, :, :], AX.X, ALU.add))
                elif what == "moments0":
                    g = i + 1
                    step = chains["x"]
                    dve.wait_ge(s_pf, GM * (g + 1))
                    nc.vector.memset(tmp0[:, :], 0.0)
                    moments(step, st0, mv0, tmp0)
                    step.then(nc.vector.tensor_tensor(mv0[:, :, 1], mv0[:, :, 1], tmp0[:, :], ALU.add))
                    step.then(nc.vector.tensor_copy(hx[:, 1, :], mv0[:, :, 0]))
                    in_parts(step, mv0, tmp0, mp0).then_inc(s_m0, 1)
                elif what == "norm0":
                    g = i + 1
                    step = chains["x"]
                    dve.wait_ge(s_g0, g + 1)
                    wait(dve, s_br, g)
                    joined(step, gs0, stat_ps)
                    step.then(nc.vector.tensor_copy(padv[:, :, 0], gs0[:, :, 0]))
                    step.then(nc.vector.tensor_tensor(padv[:, :, 1], gs0[:, :, 0], padv[:, :, 0], ALU.subtract))
                    step.then(nc.vector.tensor_tensor(var0[:, :], gs0[:, :, 0], gs0[:, :, 0], ALU.mult))
                    step.then(nc.vector.tensor_tensor(var0[:, :], gs0[:, :, 1], var0[:, :], ALU.subtract))
                    nc.vector.tensor_scalar(var0[:, :], var0[:, :], 0.0, EPS, ALU.max, ALU.add).then_inc(s_v0, 1)
                    step.then(nc.vector.tensor_tensor(hx[:, 1, :], hx[:, 1, :], gs0[:, :, 0], ALU.subtract))
                    step.then(nc.vector.tensor_tensor(hx[:, 0, :], hx[:, 1, :], lost[:, :], ALU.subtract))
                    step.then(nc.vector.scalar_tensor_tensor(hx[:, 0, :], gs0[:, :, 0], k("lost_share"),
                                                             hx[:, 0, :], ALU.mult, ALU.add))
                    dve.wait_ge(s_r0, g + 1)
                    step2 = Steps(dve, s_ch, XH, g)
                    newton(step2, var0, rs0, tmp0)
                    for s in range(2):
                        ins = nc.vector.tensor_tensor(hx[:, s, :], hx[:, s, :], rs0[:, :], ALU.mult)
                    ins.then_inc(s_hx, 1)
                    step2(nc.vector.scalar_tensor_tensor(sd0[:, :], var0[:, :], WS, rs0[:, :], ALU.mult,
                                                         ALU.mult))
                    step.end()
                    chains["gelu"] = step2
                elif what == "hidden":
                    step = chains["gelu"]
                    dve.wait_ge(s_h, i + 2)
                    step.then(nc.vector.tensor_tensor(hp[:, 0:1], h_ps, hconst[:, :], ALU.add))
                    step.then(nc.vector.tensor_scalar(hp[:, 1:2], hp[:, 0:1], 0.5 ** 0.5, 4.0, ALU.mult, ALU.min))
                    step.then(nc.vector.tensor_scalar(hp[:, 1:2], hp[:, 1:2], -4.0, None, ALU.max))
                    step.then(nc.vector.tensor_tensor(hp[:, 2:3], hp[:, 1:2], hp[:, 1:2], ALU.mult))
                    coef = k("erf", CQ).rearrange("p (k s) -> p k s", s=2)
                    src = coef[:, 0, :]
                    for t in range(1, len(ERF_TOP)):
                        ins = nc.vector.scalar_tensor_tensor(ef[:, :], src, hp[:, 2:3], coef[:, t, :],
                                                             ALU.mult, ALU.add)
                        ins.then_inc(s_erf, 1)
                        dve.wait_ge(s_erf, (len(ERF_TOP) - 1) * (i + 1) + t)
                        src = ef[:, :]
                    step.then(nc.vector.reciprocal(hp[:, 3:4], ef[:, 1:2]))
                    step.then(nc.vector.tensor_tensor(hp[:, 4:5], ef[:, 0:1], hp[:, 1:2], ALU.mult))
                    step.then(nc.vector.tensor_tensor(hp[:, 4:5], hp[:, 4:5], hp[:, 3:4], ALU.mult))
                    step.then(nc.vector.tensor_scalar(hp[:, 4:5], hp[:, 4:5], 1.0, 0.5, ALU.add, ALU.mult))
                    step.then(nc.vector.tensor_tensor(gel[:, :], hp[:, 4:5], hp[:, 0:1], ALU.mult))
                    step.then(nc.vector.tensor_copy(gel16[:, 0:1], gel[:, :]))
                    nc.vector.tensor_tensor(gel16[:, 1:2], gel[:, :], gel16[:, 0:1], ALU.subtract).then_inc(s_gel, 1)
                    step.end()
                elif what == "gate":
                    step = Steps(dve, s_ca, XA, i + 1)
                    dve.wait_ge(s_a, i + 2)
                    step.then(nc.vector.tensor_reduce(al[:, :, :], a_ps, AX.X, ALU.add))
                    step.then(nc.vector.scalar_tensor_tensor(al[:, :, :], al[:, :, :], 1.0 / WS, br2[:, :, :],
                                                             ALU.mult, ALU.add))
                    step.then(nc.vector.tensor_reduce(mx[:, :], al[:, :, :], AX.X, ALU.max))
                    for s in range(3):
                        ins = nc.vector.tensor_tensor(al[:, :, s], al[:, :, s], mx[:, :], ALU.subtract)
                    ins.then_inc(s_am, 1)
                    dve.wait_ge(s_ae, i + 2)
                    step(nc.vector.tensor_reduce(sm[:, :], al[:, :, :], AX.X, ALU.add))
                    step.then(nc.vector.tensor_tensor(gA[:, :], al[:, :, 0], al[:, :, 1], ALU.add))
                    step.then(nc.vector.reciprocal(sm[:, :], sm[:, :]))
                    nc.vector.scalar_tensor_tensor(gA[:, :], gA[:, :], WS, sm[:, :], ALU.mult, ALU.mult)
                    nc.vector.scalar_tensor_tensor(gB[:, :], al[:, :, 2], WS, sm[:, :], ALU.mult,
                                                   ALU.mult).then_inc(s_g, 1)
                    dve.wait_ge(s_g, i + 2)
                    step(nc.vector.tensor_tensor(u[:, :], gA[:, :], cols[:, 0, :], ALU.mult))
                    step.then(nc.vector.tensor_tensor(u2[:, :], gB[:, :], cols[:, 1, :], ALU.mult))
                    step.then(nc.vector.tensor_tensor(u[:, :], u[:, :], u2[:, :], ALU.add))
                    step.then(nc.vector.tensor_copy(u16[:, :, 0], u[:, :]))
                    step(nc.vector.tensor_tensor(u16[:, :, 1], u[:, :], u16[:, :, 0], ALU.subtract))
                    step.end()
                elif what == "bias":
                    dve.wait_ge(s_b, i + 2)
                    wait(dve, s_yb, KT * (i + 1))
                    nc.vector.tensor_reduce(bsum[:, :], b_ps, AX.X, ALU.add).then_inc(s_bs, 1)
                    dve.wait_ge(s_bs, 2 * (i + 2) - 1)
                    nc.vector.scalar_tensor_tensor(bsum[:, :], bsum[:, :], 1.0 / (WS * WS), cols[:, 2, :],
                                                   ALU.mult, ALU.add).then_inc(s_bs, 1)
                    dve.wait_ge(s_bs, 2 * (i + 2))
                    nc.vector.tensor_tensor(bsum[:, :], bsum[:, :], gs0[:, :, 0], ALU.add).then_inc(s_br, 1)
                elif what == "fold":
                    m = ps_m[(c + 1) % 2]
                    if c >= KT:
                        dve.wait_ge(s_f, NF * i + c + 1)
                        kt = c - KT
                        d = m[:, kt * P:(kt + 1) * P]
                        nc.vector.scalar_tensor_tensor(d, ident, sd0[:, kt:kt + 1], d, ALU.mult,
                                                       ALU.add).then_inc(s_fd, 1)
                    dve.wait_ge(s_fh, NF * i + c + 1)
                    nc.vector.scalar_tensor_tensor(w16[:, c, 1, :], m[:, 0:C], rs0[:, c % KT:c % KT + 1],
                                                   w16[:, c, 0, :], ALU.mult, ALU.subtract).then_inc(s_fl, 1)
                elif what == "keep":
                    m = KT * c + n
                    if c == 0:
                        dve.wait_ge(s_mm, GM * i + m + 1)
                        wait(dve, s_me, GM * i)
                        dve.wait_ge(s_br, i + 1)
                        nc.vector.tensor_scalar(yb[:, n:n + 1], ps_m[m % 2][:, 0:1], -1.0 / WS, bsum[:, n:n + 1],
                                                ALU.mult, ALU.add).then_inc(s_yb, 1)
                    dve.wait_ge(s_me, GM * i + m + 1)
                    nc.vector.bn_stats(st1[:, n, c, :], x1_rows(n, c)).then_inc(s_st1, 1)
                elif what == "moments1":
                    j = i - 1
                    step = Steps(dve, s_c1, XG1, j)
                    dve.wait_ge(s_st1, GM * (j + 1))
                    nc.vector.memset(tmp1[:, :], 0.0)
                    moments(step, st1, mv1, tmp1)
                    step.then(nc.vector.tensor_tensor(mv1[:, :, 1], mv1[:, :, 1], tmp1[:, :], ALU.add))
                    in_parts(step, mv1, tmp1, mp1).then_inc(s_m1, 1)
                    chains["x1"] = step
                elif what == "norm1":
                    j = i - 1
                    step = chains["x1"]
                    dve.wait_ge(s_g1, j + 1)
                    joined(step, gs1, stat1_ps)
                    step.then(nc.vector.tensor_tensor(var1[:, :], gs1[:, :, 0], gs1[:, :, 0], ALU.mult))
                    step.then(nc.vector.tensor_tensor(var1[:, :], gs1[:, :, 1], var1[:, :], ALU.subtract))
                    nc.vector.tensor_scalar(var1[:, :], var1[:, :], 0.0, EPS, ALU.max, ALU.add).then_inc(s_v1, 1)
                    dve.wait_ge(s_r1, j + 1)
                    newton(step, var1, rs1, tmp1)
                    step.then(nc.vector.tensor_tensor(nb1[:, :], gs1[:, :, 0], rs1[:, :], ALU.mult))
                    step(nc.vector.tensor_scalar(nb1[:, :], nb1[:, :], -1.0, None, ALU.mult))
                    step.settle()
                    step.end()
                elif what == "sums":
                    j = i - 1
                    done = CT * j + c
                    dve.wait_ge(s_xg, KT * (done + 1))
                    wait(dve, s_lo, 2 * (CT * j + max(0, c - 1)))
                    nc.vector.tensor_tensor_scan(rsum[:, c % 2, :], xg[:, c % 2, LEAD:LEAD + SLAB],
                                                 xg[:, c % 2, 0:SLAB], 0.0, ALU.add, ALU.subtract).then_inc(s_s, 1)
                elif what == "normalise" and c < BY_DVE:
                    j = i - 1
                    wait(dve, s_s, CT * j + max(0, c - 1))
                    wait(dve, s_q, CT * j + max(0, c - 1))
                    normalise(nc.vector, c)
                elif what == "square_sums":
                    dve.wait_ge(s_q, CT * (i - 1) + c + 1)
                    nc.vector.tensor_tensor_scan(qsum[:, c % 2, :], xq[:, LEAD:LEAD + SLAB], xq[:, 0:SLAB],
                                                 0.0, ALU.add, ALU.subtract).then_inc(s_qw, 1)
                elif what == "finish":
                    j, n = i - 1, c % TILES
                    done = CT * j + c
                    dve.wait_ge(s_num, done + 1)
                    dve.wait_ge(s_rec, done + 1)
                    wait(dve, s_st[n], 2 * 16 * (CHUNKS * j + c // TILES))
                    nc.vector.scalar_tensor_tensor(outb[:, n, :], ps_num[n % 2][0:OPX, 0:C], TINY,
                                                   rec[:, n % 2, :], ALU.add, ALU.mult).then_inc(s_rat, 1)
                    dve.wait_ge(s_xp, done + 1)
                    dve.wait_ge(s_rat, done + 1)
                    nc.vector.tensor_tensor(outb[:, n, :], ps_x1[n % 2][0:OPX, 0:C], outb[:, n, :],
                                            ALU.add).then_inc(s_out, 1)

            rounds(dve, do)

        @block.tensor
        def _(pe):
            pe.wait_ge(s_const, 32)
            pe.wait_ge(s_w, 16 * 10)
            for n in range(2 * KT):
                src = (wh_in, wc_in)[n // KT]
                wait(pe, s_sTc, n - 1)
                for t in range(KT):
                    last = nc.tensor.transpose(ps_m[n % 2][:, t * P:(t + 1) * P],
                                               src[:, t, (n % KT) * P:(n % KT + 1) * P], ident)
                last.then_inc(s_sT, 1)
            pe.wait_ge(s_sTc, 2 * KT)
            for n in range(2 * KT):
                src = (whT, wcT)[n // KT]
                wait(pe, s_sRc, n - 1 + 2)
                for t in range(KT):
                    last = nc.tensor.matmul(ps_num[n % 2][:, 0:CQ], src[:, t, (n % KT) * P:(n % KT + 1) * P],
                                            wr1[:, t, :], start=(t == 0), stop=(t == KT - 1))
                last.then_inc(s_sR, 1)
            pe.wait_ge(s_sRc, 2)
            for t in range(KT):
                last = nc.tensor.matmul(ps_x1[0][0:CQ, 0:1], wr1[:, t, :], tmp0[:, t:t + 1],
                                        start=(t == 0), stop=(t == KT - 1))
            last.then_inc(s_sR, 1)
            pe.wait_ge(s_sRc, 2 * KT + 4)
            pe.wait_ge(s_gap, 1)

            def group_moments(dst, mp):
                for m in range(KT):
                    near = [t for t in range(KT) if abs(t - m) <= 1]
                    for t in near:
                        last = nc.tensor.matmul(dst[:, m, :], k16(f"group{t}{m}"),
                                                mp[:, t, :, :].rearrange("p k s -> p (k s)"),
                                                start=(t == near[0]), stop=(t == near[-1]))
                return last

            def do(it, i):
                what, c, n = it
                if what == "read":
                    img = i + 1
                    m = GM * img + KT * c + n
                    if n == 0:
                        slot = c % 2
                        per = (CHUNKS + 1 - slot) // 2
                        pe.wait_ge(s_x[slot], 16 * (per * img + c // 2 + 1))
                        if c == 0:
                            wait(pe, s_br, img)
                    wait(pe, s_pf, m - 1 if isinstance(i, int) and i < 0 else m)
                    for t in range(TILES):
                        last = nc.tensor.transpose(read_bank(i, KT * c + n)[:, t * TPX:(t + 1) * TPX],
                                                   xin[c % 2][:, t, n * P:(n + 1) * P], ident[0:TPX, 0:TPX])
                    last.then_inc(s_p, 1)
                elif what == "norm0":
                    pe.wait_ge(s_m0, i + 2)
                    pe.wait_ge(s_pf, GM * (i + 2))
                    group_moments(stat_ps, mp0).then_inc(s_g0, 1)
                elif what == "norm1":
                    pe.wait_ge(s_m1, i)
                    wait(pe, s_out, CT * (i - 1))
                    group_moments(stat1_ps, mp1).then_inc(s_g1, 1)
                elif what == "hidden":
                    pe.wait_ge(s_hx, i + 2)
                    for s, r in enumerate((r_h, r_c)):
                        for t in range(KT):
                            last = nc.tensor.matmul(h_ps, r[:, t, :], hx[:, s, t:t + 1],
                                                    start=(s == 0 and t == 0), stop=(s == 1 and t == KT - 1))
                    last.then_inc(s_h, 1)
                elif what == "gate":
                    pe.wait_ge(s_gel, i + 2)
                    for m in range(KT):
                        w = wr16[:, :, m * 3 * P:(m + 1) * 3 * P].rearrange("p k (c s) -> p k c s", s=3)
                        for s in range(3):
                            for part in range(2):
                                last = nc.tensor.matmul(a_ps[:, m, s, :], w[:, part, :, s], gel16[:, :],
                                                        start=(part == 0), stop=(part == 1))
                    last.then_inc(s_a, 1)
                elif what == "bias":
                    pe.wait_ge(s_ca, XA * (i + 2))
                    for m in range(KT):
                        terms = [(t, part) for t in range(KT) for part in range(2)]
                        for n, (t, part) in enumerate(terms):
                            last = nc.tensor.matmul(b_ps[:, m, :], wp16[:, t, part, m * P:(m + 1) * P], u16[:, t, :],
                                                    start=(n == 0), stop=(n == len(terms) - 1))
                    last.then_inc(s_b, 1)
                elif what == "fold":
                    pe.wait_ge(s_wA, 2 * KT * i + (KT if c < KT else 2 * KT))
                    if c < 2:
                        wait(pe, s_me, GM * i - 1 + c)
                    else:
                        pe.wait_ge(s_fl, NF * i + c - 1)
                    left, right = (whT, wA) if c < KT else (wcT, wB)
                    for t in range(KT):
                        last = nc.tensor.matmul(ps_m[(c + 1) % 2][:, 0:C], left[:, t, (c % KT) * P:(c % KT + 1) * P],
                                                right[:, t, :], start=(t == 0), stop=(t == KT - 1))
                    last.then_inc(s_f, 1)
                elif what == "project":
                    m = KT * c + n
                    if m < 2:
                        pe.wait_ge(s_fl, NF * (i + 1))
                    else:
                        pe.wait_ge(s_me, GM * i + m - 1)
                    if n == 0:
                        nth = sum(1 for e in range(c) if SLOT[e] == SLOT[c])
                        pe.wait_ge(s_sh[SLOT[c]], 16 * NRES * (USES[SLOT[c]] * i + nth + 1))
                        if c == 0:
                            pe.wait_ge(s_pad, i + 1)
                    e = 1 if c == 0 else 0
                    a = HALO + c * CPX
                    terms = [(f, wpart, xpart) for f in range(NF) for wpart, xpart in ((0, 0), (1, 0), (0, 1))]
                    for t, (f, wpart, xpart) in enumerate(terms):
                        kt = f % KT
                        rhs = (sh[:, SLOT[c], kt, xpart, 2 - e:2 + CPX] if f < KT
                               else hl[:, kt, xpart, a - e:a + CPX])
                        last = nc.tensor.matmul(ps_m[m % 2][:, 0:CPX + e], w16[:, f, wpart, n * P:(n + 1) * P],
                                                rhs, start=(t == 0), stop=(t == len(terms) - 1))
                    last.then_inc(s_mm, 1)
                elif what == "tile":
                    j, n = i - 1, c % TILES
                    done = CT * j + c
                    pe.wait_ge(s_lo, 2 * (done + 1))
                    for src, dst, ready in ((qsp, ps_den, s_den), (rsp, ps_num[n % 2], s_num)):
                        if dst is ps_den:
                            wait(pe, s_ln, done)
                        else:
                            wait(pe, s_rat, CT * j + max(0, c - 1))
                        for t, (lo, hi) in enumerate(BANDS):
                            a = 2 * t * PITCH + 2
                            for part in range(2):
                                last = nc.tensor.matmul(dst[0:OPX, lo:hi], src[:, c % AHEAD, part, a:a + OPX],
                                                        k16(f"band{t}"), start=(t == 0 and part == 0),
                                                        stop=(t == KT - 1 and part == 1), skip_group_check=True)
                        last.then_inc(ready, 1)
                    wait(pe, s_out, CT * j + max(0, c - 1))
                    if c == 0:
                        pe.wait_ge(s_v1, j + 1)
                    a = 2 * c * PITCH
                    for t in range(KT):
                        last = nc.tensor.transpose(ps_x1[n % 2][0:OPX, t * P:(t + 1) * P], x1T[:, t, a:a + OPX],
                                                   ident)
                    last.then_inc(s_xp, 1)

            rounds(pe, do)


def kernel(x, L0_conv_w_h, L0_conv_b_h, L0_conv_w_c, L0_conv_b_c, L0_conv_w_r1, L0_conv_b_r1, L0_conv_w_r2,
           L0_conv_b_r2, L0_conv_w_p, L0_conv_b_p):
    import concourse.bacc as bacc
    from concourse.bass_utils import run_bass_kernel_spmd

    g = geometry(x.shape)
    (blob, ones), at = constant_blob(g)
    nc = bacc.Bacc("TRN2", target_bir_lowering=False, num_devices=1)
    given = dict(x=x, w_h=L0_conv_w_h, b_h=L0_conv_b_h, w_c=L0_conv_w_c, b_c=L0_conv_b_c, w_r1=L0_conv_w_r1,
                 b_r1=L0_conv_b_r1, w_r2=L0_conv_w_r2, b_r2=L0_conv_b_r2, w_p=L0_conv_w_p, b_p=L0_conv_b_p,
                 blob=blob, ones=ones)
    arrays, args = {}, {}
    for name, a in given.items():
        a = np.ascontiguousarray(a)
        arrays[f"in_{name}"] = a
        args[name] = nc.dram_tensor(f"in_{name}", a.shape, mybir.dt.from_np(a.dtype), kind="ExternalInput").ap()
    args["out"] = nc.dram_tensor("out_x", x.shape, mybir.dt.float32, kind="ExternalOutput").ap()
    build(nc, g, at, **args)
    return run_bass_kernel_spmd(nc, [arrays], core_ids=[0]).results[0]["out_x"]
```
